# Optimizing a Trainium2 kernel written in Bass

```python
import numpy as np
import jax
import jax.numpy as jnp

def _softmax(x, axis=-1):
    return jax.nn.softmax(x, axis=axis)

def _gelu(x):
    return jax.nn.gelu(x, approximate=True)

def _silu(x):
    return jax.nn.silu(x)

def _sigmoid(x):
    return jax.nn.sigmoid(x)

def _layernorm(x, axis=-1, eps=1e-05):
    m = jnp.mean(x, axis=axis, keepdims=True)
    v = jnp.var(x, axis=axis, keepdims=True)
    return (x - m) / jnp.sqrt(v + eps)

def _scatter_add(tgt, idx, src, axis=0):
    return tgt.at[idx].add(src)

def _segment_sum(src, seg, n):
    return jax.ops.segment_sum(src, seg, n)
kernel_name = 'mk_adaln_d1_jaxref_r4_52799d'

def setup_inputs(seed: int=0):
    np.random.seed(seed)
    _w = jnp.asarray

    def _L0_attn_setup():
        import jax, jax.numpy as jnp
        import numpy as np
        EPS = 1e-06
        CHUNK = 64
        N_HEADS = 16
        GATE_NORM = 16.0

        def rmsnorm(x, eps=EPS):
            return x * jax.lax.rsqrt(jnp.mean(x * x, axis=-1, keepdims=True) + eps)

        def chunk_gate_retention(q, k, v, gt, chunk_size):
            b, h, t, d = q.shape
            c = chunk_size
            n = t // c
            scale = d ** (-0.5)
            q = q.reshape(b, h, n, c, d) * scale
            k = k.reshape(b, h, n, c, d)
            v = v.reshape(b, h, n, c, d)
            g = gt.reshape(b, h, n, c)
            bc = jnp.cumsum(g, axis=-1)
            B = bc[..., -1:]
            decay = jnp.exp(bc[..., :, None] - bc[..., None, :])
            mask = jnp.tril(jnp.ones((c, c), dtype=bool))
            A = jnp.einsum('bhnid,bhnjd->bhnij', q, k) * jnp.where(mask, decay, 0.0)
            o_intra = jnp.einsum('bhnij,bhnjd->bhnid', A, v)
            kd = k * jnp.exp(B - bc)[..., None]
            kv = jnp.einsum('bhncd,bhnce->bhnde', kd, v)
            qd = q * jnp.exp(bc)[..., None]

            def step(S, inp):
                qd_n, kv_n, B_n = inp
                o_cross = jnp.einsum('bhcd,bhde->bhce', qd_n, S)
                S_new = jnp.exp(B_n)[..., None] * S + kv_n
                return (S_new, o_cross)
            S0 = jnp.zeros((b, h, d, d), dtype=q.dtype)
            inps = (jnp.moveaxis(qd, 2, 0), jnp.moveaxis(kv, 2, 0), jnp.moveaxis(B, 2, 0))
            S_last, o_cross = jax.lax.scan(step, S0, inps)
            o_cross = jnp.moveaxis(o_cross, 0, 2)
            o = (o_intra + o_cross).reshape(b, h, t, d)
            return (o, S_last)
        key = jax.random.key(seed)
        ks = jax.random.split(key, 7)
        dim, nh = (256, N_HEADS)
        s = 0.03
        return {'x': jax.random.normal(ks[0], (2, 2048, dim), dtype=jnp.float32), 'Wq': jax.random.normal(ks[1], (dim, dim), dtype=jnp.float32) * s, 'Wk': jax.random.normal(ks[2], (dim, dim), dtype=jnp.float32) * s, 'Wv': jax.random.normal(ks[3], (dim, dim), dtype=jnp.float32) * s, 'Wg': jax.random.normal(ks[4], (dim, dim), dtype=jnp.float32) * s, 'Wgt': jax.random.normal(ks[5], (dim, nh), dtype=jnp.float32) * s, 'Wo': jax.random.normal(ks[6], (dim, dim), dtype=jnp.float32) * s}
    _L0_attn_in = _L0_attn_setup()

    def _L0_ffn_setup():
        import jax, jax.numpy as jnp
        import numpy as np
        DIM = 256

        def _reference_tuple_inner(x, W_r, W_k, W_v, mu_r, mu_k):
            B, T, C = x.shape
            x_prev = jnp.concatenate([jnp.zeros((B, 1, C), x.dtype), x[:, :-1, :]], axis=1)
            xr = mu_r * x + (1.0 - mu_r) * x_prev
            xk = mu_k * x + (1.0 - mu_k) * x_prev
            r = jax.nn.sigmoid(jnp.einsum('btc,dc->btd', xr, W_r))
            k = jnp.einsum('btc,dc->btd', xk, W_k)
            k_act = jnp.square(jax.nn.relu(k))
            out = r * jnp.einsum('btc,dc->btd', k_act, W_v)
            new_state = x[:, -1, :]
            return (out, new_state)
        key = jax.random.key(seed)
        ks = jax.random.split(key, 6)
        B, T, C = (8, 512, DIM)
        x = jax.random.normal(ks[0], (B, T, C), dtype=jnp.float32)
        s = 1.0 / np.sqrt(C)
        W_r = jax.random.uniform(ks[1], (C, C), jnp.float32, -s, s)
        W_k = jax.random.uniform(ks[2], (C, C), jnp.float32, -s, s)
        W_v = jax.random.uniform(ks[3], (C, C), jnp.float32, -s, s)
        mu_r = jax.random.uniform(ks[4], (C,), jnp.float32)
        mu_k = jax.random.uniform(ks[5], (C,), jnp.float32)
        return {'x': x, 'W_r': W_r, 'W_k': W_k, 'W_v': W_v, 'mu_r': mu_r, 'mu_k': mu_k}
    _L0_ffn_in = _L0_ffn_setup()
    _L0_c = _w((lambda *s: np.random.randn(*s).astype(np.float32) * 0.05)(16, 256))
    _L0_wmod = _w((lambda *s: np.random.randn(*s).astype(np.float32) * 0.05)(256, 6 * 256) * 256 ** (-0.5))
    _d = {'L0_attn_x': _L0_attn_in['x'], 'L0_attn_Wq': _L0_attn_in['Wq'], 'L0_attn_Wk': _L0_attn_in['Wk'], 'L0_attn_Wv': _L0_attn_in['Wv'], 'L0_attn_Wg': _L0_attn_in['Wg'], 'L0_attn_Wgt': _L0_attn_in['Wgt'], 'L0_attn_Wo': _L0_attn_in['Wo'], 'L0_ffn_W_r': _L0_ffn_in['W_r'], 'L0_ffn_W_k': _L0_ffn_in['W_k'], 'L0_ffn_W_v': _L0_ffn_in['W_v'], 'L0_ffn_mu_r': _L0_ffn_in['mu_r'], 'L0_ffn_mu_k': _L0_ffn_in['mu_k'], 'L0_c': _L0_c, 'L0_wmod': _L0_wmod}
    _x0 = _d['L0_attn_x']
    _d['L0_attn_x'] = jax.random.normal(jax.random.fold_in(jax.random.key(seed), 1), (16, 512, 256), dtype=_x0.dtype)
    del _x0
    return _d

def reference(L0_attn_x, L0_attn_Wq, L0_attn_Wk, L0_attn_Wv, L0_attn_Wg, L0_attn_Wgt, L0_attn_Wo, L0_ffn_W_r, L0_ffn_W_k, L0_ffn_W_v, L0_ffn_mu_r, L0_ffn_mu_k, L0_c, L0_wmod):

    def _L0_attn_ref(x, Wq, Wk, Wv, Wg, Wgt, Wo):
        import jax, jax.numpy as jnp
        import numpy as np
        EPS = 1e-06
        CHUNK = 64
        N_HEADS = 16
        GATE_NORM = 16.0

        def rmsnorm(x, eps=EPS):
            return x * jax.lax.rsqrt(jnp.mean(x * x, axis=-1, keepdims=True) + eps)

        def chunk_gate_retention(q, k, v, gt, chunk_size):
            b, h, t, d = q.shape
            c = chunk_size
            n = t // c
            scale = d ** (-0.5)
            q = q.reshape(b, h, n, c, d) * scale
            k = k.reshape(b, h, n, c, d)
            v = v.reshape(b, h, n, c, d)
            g = gt.reshape(b, h, n, c)
            bc = jnp.cumsum(g, axis=-1)
            B = bc[..., -1:]
            decay = jnp.exp(bc[..., :, None] - bc[..., None, :])
            mask = jnp.tril(jnp.ones((c, c), dtype=bool))
            A = jnp.einsum('bhnid,bhnjd->bhnij', q, k) * jnp.where(mask, decay, 0.0)
            o_intra = jnp.einsum('bhnij,bhnjd->bhnid', A, v)
            kd = k * jnp.exp(B - bc)[..., None]
            kv = jnp.einsum('bhncd,bhnce->bhnde', kd, v)
            qd = q * jnp.exp(bc)[..., None]

            def step(S, inp):
                qd_n, kv_n, B_n = inp
                o_cross = jnp.einsum('bhcd,bhde->bhce', qd_n, S)
                S_new = jnp.exp(B_n)[..., None] * S + kv_n
                return (S_new, o_cross)
            S0 = jnp.zeros((b, h, d, d), dtype=q.dtype)
            inps = (jnp.moveaxis(qd, 2, 0), jnp.moveaxis(kv, 2, 0), jnp.moveaxis(B, 2, 0))
            S_last, o_cross = jax.lax.scan(step, S0, inps)
            o_cross = jnp.moveaxis(o_cross, 0, 2)
            o = (o_intra + o_cross).reshape(b, h, t, d)
            return (o, S_last)
        b, t, dim = x.shape
        h = N_HEADS
        d = dim // h
        q = rmsnorm(x @ Wq)
        k = rmsnorm(x @ Wk)
        v = rmsnorm(x @ Wv)
        g = x @ Wg
        gt = jax.nn.log_sigmoid(x @ Wgt) / GATE_NORM
        qr = q.reshape(b, t, h, d).transpose(0, 2, 1, 3)
        kr = k.reshape(b, t, h, d).transpose(0, 2, 1, 3)
        vr = v.reshape(b, t, h, d).transpose(0, 2, 1, 3)
        gtr = gt.transpose(0, 2, 1)
        o, _ = chunk_gate_retention(qr, kr, vr, gtr, CHUNK)
        o = rmsnorm(o)
        o = o.transpose(0, 2, 1, 3).reshape(b, t, dim)
        o = jax.nn.silu(g) * o
        return o @ Wo

    def _L0_ffn_ref(x, W_r, W_k, W_v, mu_r, mu_k):
        import jax, jax.numpy as jnp
        import numpy as np
        DIM = 256

        def _reference_tuple_inner(x, W_r, W_k, W_v, mu_r, mu_k):
            B, T, C = x.shape
            x_prev = jnp.concatenate([jnp.zeros((B, 1, C), x.dtype), x[:, :-1, :]], axis=1)
            xr = mu_r * x + (1.0 - mu_r) * x_prev
            xk = mu_k * x + (1.0 - mu_k) * x_prev
            r = jax.nn.sigmoid(jnp.einsum('btc,dc->btd', xr, W_r))
            k = jnp.einsum('btc,dc->btd', xk, W_k)
            k_act = jnp.square(jax.nn.relu(k))
            out = r * jnp.einsum('btc,dc->btd', k_act, W_v)
            new_state = x[:, -1, :]
            return (out, new_state)
        return _reference_tuple_inner(x, W_r, W_k, W_v, mu_r, mu_k)[0]
    x = L0_attn_x
    mod = (_silu(L0_c) @ L0_wmod).reshape(L0_c.shape[0], 6, 1, -1)
    sa, ca, ga, sb, cb, gb = (mod[:, 0], mod[:, 1], mod[:, 2], mod[:, 3], mod[:, 4], mod[:, 5])
    ga = (2 * (ga >= 0) - 1) * jnp.maximum(jnp.abs(ga), 0.25)
    gb = (2 * (gb >= 0) - 1) * jnp.maximum(jnp.abs(gb), 0.25)
    h = _layernorm(x, axis=-1) * (1 + ca) + sa
    x = x + ga * _L0_attn_ref(h, L0_attn_Wq, L0_attn_Wk, L0_attn_Wv, L0_attn_Wg, L0_attn_Wgt, L0_attn_Wo)
    h = _layernorm(x, axis=-1) * (1 + cb) + sb
    x = x + gb * _L0_ffn_ref(h, L0_ffn_W_r, L0_ffn_W_k, L0_ffn_W_v, L0_ffn_mu_r, L0_ffn_mu_k)
    return x

_drawn_inputs = setup_inputs


def setup_inputs(seed=0):
    import zlib

    import numpy as np

    out = dict(_drawn_inputs(seed))
    spreads = {}
    factors = {'L0_attn_Wgt': 32.672,
     'L0_ffn_W_r': 8.0,
     'L0_ffn_W_k': 3.018,
     'L0_ffn_W_v': 2.766,
     'L0_ffn_mu_r': 8.0,
     'L0_ffn_mu_k': 5.001}
    for name, (base, spread) in spreads.items():
        noise = np.random.default_rng([zlib.crc32(name.encode()), seed]).standard_normal(out[name].shape)
        drawn = base * np.exp(spread * noise) if base else spread * noise
        out[name] = jnp.asarray(drawn.astype(out[name].dtype))
    for name, factor in factors.items():
        out[name] = (out[name] * factor).astype(out[name].dtype)
    return out
```

```python
from contextlib import ExitStack

import concourse.bass as bass
from concourse import mybir

ALU = mybir.AluOpType
ACT = mybir.ActivationFunctionType
F32 = mybir.dt.float32
BF16 = mybir.dt.bfloat16

P = 128
BANK = 512
HEADS = 16
CHUNK = 64
GATE_NORM = 16.0
LN_EPS = 1e-5
RMS_EPS = 1e-6
MIN_GATE = 0.25
MASKED = -1e38


def adaln_block(nc, x, Wq, Wk, Wv, Wg, Wgt, Wo, WrT, WkT, WvT, mu_r, mu_k, cT, wmod, out):
    B, T, D = x.shape
    HALVES = D // P
    TILES = T // P
    CHUNKS = T // CHUNK
    DH = D // HEADS
    HPH = HEADS // HALVES
    PAIRS = P // 32
    NM = 6 * HALVES
    assert (HALVES, TILES, DH, T, P // CHUNK) == (2, 4, 16, BANK, 2)

    mod_dram = nc.dram_tensor("mod_scratch", (B, P, 8), F32, kind="Internal").ap()
    gate_dram = nc.dram_tensor("gate_scratch", (B, 2 * D), F32, kind="Internal").ap()
    x_tiles = x.rearrange("b (t p) d -> b p t d", p=P)
    out_tiles = out.rearrange("b (t p) d -> b p t d", p=P)

    with ExitStack() as ctx:
        def sb(name, shape, dt=F32):
            return ctx.enter_context(nc.sbuf_tensor(name, shape, dt))

        def sem(name):
            return ctx.enter_context(nc.semaphore(name))

        w_q, w_k, w_v, w_g, w_o, w_r, w_fk, w_fv, w_o_gated, w_fv_gated = (
            sb(n, [P, HALVES, D]) for n in
            ("w_q", "w_k", "w_v", "w_g", "w_o", "w_r", "w_fk", "w_fv", "w_o_gated", "w_fv_gated"))
        w_gt16 = sb("w_gt16", [P, HALVES, HEADS])
        w_gt = sb("w_gt", [P, HALVES, 8, HEADS])
        mu = sb("mu", [P, 2, HALVES])
        ident = sb("ident", [P, P])
        ident_bf = sb("ident_bf", [P, P], BF16)
        causal = sb("causal", [P, HPH, CHUNK], BF16)
        causal1 = sb("causal1", [P, CHUNK], BF16)
        head_sel = sb("head_sel", [P, D], BF16)
        head_sel_neg = sb("head_sel_neg", [P, HEADS], BF16)
        lhs_scale = sb("lhs_scale", [P, 1])
        lhs_shift = sb("lhs_shift", [P, 1])
        head_mean = sb("head_mean", [P, P])
        head_block = sb("head_block", [P, 32])
        eps_mean = sb("eps_mean", [P, P])
        chunk_keep = sb("chunk_keep", [P, T])
        eps_ln = sb("eps_ln", [P, 1])
        eps_rms = sb("eps_rms", [P, 1])
        eps_out = sb("eps_out", [P, 1])
        one = sb("one", [P, 1])
        carrier = sb("carrier", [P, 1])

        x_in = sb("x_in", [P, TILES, D])
        mod_a = sb("mod_a", [P, 4])
        gate_a = sb("gate_a", [P, D])
        ln_stats = sb("ln_stats", [P, TILES, 6])
        ln_mv = sb("ln_mv", [P, TILES, 2])
        rstd = sb("rstd", [P, TILES])
        z = sb("z", [P, TILES, D])
        hT = sb("hT", [P, HALVES, T])
        qT = sb("qT", [P, HALVES, T])
        q_diag = sb("q_diag", [P, HALVES, HPH, T])
        q_sq = sb("q_sq", [P, HALVES, T])
        q_dec = qT
        kT = sb("kT", [P, HALVES, T])
        k_dec = sb("k_dec", [P, TILES, D])
        v_pad = sb("v_pad", [P, 2, TILES, HEADS, 32])
        g_copy = sb("g_copy", [P, HALVES, T])
        g_log = sb("g_log", [P, HALVES, T])
        g_exp = sb("g_exp", [P, HALVES, T])
        gt_a = sb("gt_a", [P, T])
        gt_b = sb("gt_b", [P, T])
        chunk_end = sb("chunk_end", [P, T], BF16)
        decay_sum = sb("decay_sum", [P, T])
        split = sb("split", [P, T], BF16)
        arg_lhs = sb("arg_lhs", [P, T], BF16)
        arg_rhs = sb("arg_rhs", [P, HEADS, T], BF16)
        decay_T = sb("decay_T", [P, HALVES, T])
        k_tail = sb("k_tail", [P, TILES * HEADS])
        kv_sumsq = sb("kv_sumsq", [P, 2, TILES])
        kv_rms = sb("kv_rms", [P, TILES])
        kv_rms8 = sb("kv_rms8", [P, TILES, 8])
        kv_new = sb("kv_new", [P, HALVES, 32, CHUNKS])
        chunk_decay = sb("chunk_decay", [P, HALVES, 32, CHUNKS])
        state = sb("state", [P, HALVES, 32, CHUNKS])
        state_diag = sb("state_diag", [P, HALVES, CHUNKS, P])
        decay = sb("decay", [P, 2, HEADS * CHUNK])
        probs = sb("probs", [P, 2, HEADS * CHUNK])
        o_sq = qT
        o_gated = decay[:, 0, :].rearrange("p (a t) -> p a t", a=HALVES)
        sq_junk = decay[:, 1, :].bitcast(BF16).rearrange("p (t d) -> p t d", d=D)
        x1 = sb("x1", [P, TILES, D])
        ln2_stats = sb("ln2_stats", [P, TILES, 6])
        ln2_mv = sb("ln2_mv", [P, TILES, 2])
        rstd2 = sb("rstd2", [P, TILES])
        z2 = sb("z2", [P, TILES, D])

        mod_f = sb("mod_f", [P, 4])
        gate_f = sb("gate_f", [P, D])
        h2T = sb("h2T", [P, HALVES, T + 1])
        shift_d = sb("shift_d", [P, HALVES, T])
        act_T = shift_d
        xrT = sb("xrT", [P, HALVES, T])
        xkT = sb("xkT", [P, HALVES, T])
        r_min = sb("r_min", [P, TILES, D])
        r_exp = g_exp[:, :, :].rearrange("p a (b d) -> p (a b) d", d=D)
        ffn = r_min
        wmod_sb = q_diag[:, :, :, :].rearrange("p a h t -> p (a h t)")[:, 0:HALVES * 6 * D].rearrange(
            "p (k n) -> p k n", k=HALVES)
        cT_sb = sb("cT_sb", [P, HALVES, B])
        c_silu = sb("c_silu", [P, HALVES, B])
        c_tmp = sb("c_tmp", [P, HALVES, B])
        mod_all = z[:, :, :].rearrange("p t d -> p (t d)")[:, 0:B * 8].rearrange("p (b k) -> p b k", k=8)
        gate_rows = z2[:, :, :].rearrange("p t d -> p (t d)")[0:B, 0:2 * D]
        gate_tmp = z2[:, :, :].rearrange("p t d -> p (t d)")[0:B, 2 * D:4 * D]

        ps = ctx.enter_context(nc.psum_tensor("ps", [P, 8, BANK], F32))

        def bank(n, width=1):
            return ps[:, n:n + width, :]

        s_w = sem("weights_loaded")
        s_wmod = sem("wmod_loaded")
        s_pc = sem("pool_constants")
        s_vc = sem("vector_constants")
        s_c1 = sem("c_exp_done")
        s_c2 = sem("c_silu_steps")
        s_modp = sem("mod_product_ready")
        s_mods = sem("mod_steps")
        s_modw = sem("mod_written")
        x_loaded = sem("x_loaded")
        moda_loaded = sem("moda_loaded")
        gatea_loaded = sem("gatea_loaded")
        modf_loaded = sem("modf_loaded")
        gatef_loaded = sem("gatef_loaded")
        xres_loaded = sem("xres_loaded")
        stored = sem("stored")
        ln_stat = sem("ln_stat")
        ln_log = sem("ln_log")
        rstd_ready = sem("rstd_ready")
        z_ready = sem("z_ready")
        zT_ready = sem("zT_ready")
        hT_ready = sem("hT_ready")
        gt_ready = sem("gt_ready")
        gt_min = sem("gt_min")
        gt_nabs = sem("gt_nabs")
        gt_exp = sem("gt_exp")
        gt_log = sem("gt_log")
        gt_diff = sem("gt_diff")
        decay_scanned = sem("decay_scanned")
        split_step = sem("split_step")
        lhs_ready = sem("lhs_ready")
        chunk_end_ready = sem("chunk_end_ready")
        rhs_placed = sem("rhs_placed")
        q_ready = sem("q_ready")
        k_ready = sem("k_ready")
        g_ready = sem("g_ready")
        v_ready = sem("v_ready")
        qsq_ready = sem("qsq_ready")
        qT_ready = sem("qT_ready")
        qsum_ready = sem("qsum_ready")
        q_placed = sem("q_placed")
        kT_ready = sem("kT_ready")
        gcopy_ready = sem("gcopy_ready")
        gmin_ready = sem("gmin_ready")
        gabs_ready = sem("gabs_ready")
        gexp_ready = sem("gexp_ready")
        gln_ready = sem("gln_ready")
        gsig_ready = sem("gsig_ready")
        vsq_ready = sem("vsq_ready")
        ktok_ready = sem("ktok_ready")
        ksq_ready = sem("ksq_ready")
        kvlog_ready = sem("kvlog_ready")
        kvlog_sum = sem("kvlog_sum")
        kvrms_ready = sem("kvrms_ready")
        vpad_ready = sem("vpad_ready")
        e_ready = sem("e_ready")
        decayT_ready = sem("decayT_ready")
        tail_ready = sem("tail_ready")
        ktail_ready = sem("ktail_ready")
        kdec_ready = sem("kdec_ready")
        qdec_ready = sem("qdec_ready")
        kv_ready = sem("kv_ready")
        kvnew_ready = sem("kvnew_ready")
        cdecay_ready = sem("cdecay_ready")
        state_ready = sem("state_ready")
        sdiag_act = sem("sdiag_act")
        sdiag_pool = sem("sdiag_pool")
        arg_ready = sem("arg_ready")
        decay_ready = sem("decay_ready")
        qk_ready = sem("qk_ready")
        probs_ready = sem("probs_ready")
        pv_ready = sem("pv_ready")
        osq_ready = sem("osq_ready")
        ms_ready = sem("ms_ready")
        mslog_ready = sem("mslog_ready")
        gexpo_ready = sem("gexpo_ready")
        gfac_ready = sem("gfac_ready")
        ohalf_ready = sem("ohalf_ready")
        og_ready = sem("og_ready")
        wo_ready = sem("wo_ready")
        attn_ready = sem("attn_ready")
        x1_ready = sem("x1_ready")
        ln2_stat = sem("ln2_stat")
        ln2_log = sem("ln2_log")
        rstd2_ready = sem("rstd2_ready")
        z2_ready = sem("z2_ready")
        z2T_ready = sem("z2T_ready")
        h2T_ready = sem("h2T_ready")
        shift_ready = sem("shift_ready")
        xk0_ready = sem("xk0_ready")
        xk_ready = sem("xk_ready")
        xr_ready = sem("xr_ready")
        fk_ready = sem("fk_ready")
        relu_ready = sem("relu_ready")
        act_ready = sem("act_ready")
        fr_ready = sem("fr_ready")
        rabs_ready = sem("rabs_ready")
        rmin_ready = sem("rmin_ready")
        rexp_ready = sem("rexp_ready")
        rln_ready = sem("rln_ready")
        rsig_ready = sem("rsig_ready")
        r_ready = sem("r_ready")
        wv_ready = sem("wv_ready")
        fv_ready = sem("fv_ready")
        ffn_ready = sem("ffn_ready")
        y_ready = sem("y_ready")

        block = ctx.enter_context(nc.Block())

        def need(eng, s, per, i, k=None):
            value = per * i + (per if k is None else k)
            if isinstance(value, int) and value <= 0:
                return
            eng.wait_ge(s, value)

        def schedule(eng, body):
            body(0, True, False)
            body(1, True, True)
            with eng.Fori(2, B) as i:
                body(i, True, True)
            body(B, False, True)


        def element(dram, i):
            return dram[i:i + 1] if isinstance(i, int) else dram[bass.ds(i, 1)]

        def tokens(dram, i):
            return element(dram, i).rearrange("b p t d -> (b p) t d")

        def columns(dram, i, a, b):
            return element(dram, i)[:, :, a:b].rearrange("b p k -> (b p) k")

        def gate_row(i, a, b):
            return element(gate_dram, i)[:, a:b].rearrange("b d -> (b d)").partition_broadcast(P)

        @block.sync
        def _(sp):
            sp.dma_start(cT_sb[:], cT.rearrange("(k p) n -> p k n", p=P)).then_inc(s_wmod, 16)
            sp.dma_start(wmod_sb, wmod.rearrange("(k p) n -> p k n", p=P)).then_inc(s_wmod, 16)
            sp.dma_start(x_in[:], tokens(x_tiles, 0)).then_inc(x_loaded, 16)
            for dst, src in ((w_gt16, Wgt), (w_q, Wq), (w_k, Wk), (w_g, Wg), (w_v, Wv), (w_o, Wo),
                             (w_r, WrT), (w_fk, WkT), (w_fv, WvT)):
                sp.dma_start(dst[:], src.rearrange("(k p) n -> p k n", p=P)).then_inc(s_w, 16)
            for n, src in enumerate((mu_r, mu_k)):
                sp.dma_start(mu[:, n, :], src.rearrange("(k p) -> p k", p=P), allow_slow_non_contiguous=True).then_inc(s_w, 16)
            sp.wait_ge(s_mods, 10)
            sp.dma_start(mod_dram.rearrange("b p k -> p b k"), mod_all).then_inc(s_modw, 16)
            sp.dma_start(gate_dram, gate_rows).then_inc(s_modw, 16)
            sp.wait_ge(s_modw, 32)
            sp.dma_start(mod_a[:], columns(mod_dram, 0, 0, 4)).then_inc(moda_loaded, 16)
            sp.dma_start(gate_a[:], gate_row(0, 0, D)).then_inc(gatea_loaded, 16)
            sp.wait_ge(s_vc, VECTOR_CONSTANTS)

            def body(i, attn, later, prefetch=True):
                j = i - 1
                if attn:
                    if prefetch:
                        need(sp, z_ready, 4, i)
                        sp.dma_start(x_in[:], tokens(x_tiles, i + 1)).then_inc(x_loaded, 16)
                        need(sp, hT_ready, 2, i)
                        sp.dma_start(mod_a[:], columns(mod_dram, i + 1, 0, 4)).then_inc(moda_loaded, 16)
                    need(sp, qk_ready, 4, i - 1)
                    need(sp, qT_ready, 1, i)
                    for h in range(HPH):
                        rows = slice(DH * h, DH * (h + 1))
                        sp.dma_start(q_diag[rows, :, h, :], qT[rows, :, :]).then_inc(q_placed, 16)
                    need(sp, arg_ready, 4, i - 1)
                    need(sp, split_step, 5, i)
                    for h in range(HEADS):
                        rows = slice(HEADS + h, P, 32)
                        sp.dma_start(arg_rhs[rows, h, :], split[rows, :]).then_inc(rhs_placed, 16)
                    if prefetch:
                        need(sp, wo_ready, 1, i)
                        sp.dma_start(gate_a[:], gate_row(i + 1, 0, D)).then_inc(gatea_loaded, 16)
                    need(sp, h2T_ready, 2, j)
                    sp.dma_start(mod_f[:], columns(mod_dram, i, 4, 8)).then_inc(modf_loaded, 16)
                    need(sp, wv_ready, 1, j)
                    sp.dma_start(gate_f[:], gate_row(i, D, 2 * D)).then_inc(gatef_loaded, 16)
                if later:
                    need(sp, y_ready, 1, j)
                    sp.dma_start(tokens(out_tiles, j), ffn[:]).then_inc(stored, 16)
                if attn:
                    sp.dma_start(x1[:], tokens(x_tiles, i)).then_inc(xres_loaded, 16)

            body(0, True, False)
            body(1, True, True)
            with sp.Fori(2, B - 1) as i:
                body(i, True, True)
            body(B - 1, True, True, prefetch=False)
            body(B, False, True)
            sp.wait_ge(stored, 16 * B)

        @block.gpsimd
        def _(pool):
            g = nc.gpsimd
            g.memset(ident[:], 0.0).then_inc(s_pc, 1)
            g.memset(ident_bf[:], 0.0).then_inc(s_pc, 1)
            g.memset(causal1[:], 0.0).then_inc(s_pc, 1)
            g.memset(head_sel[:], 0.0).then_inc(s_pc, 1)
            g.memset(head_mean[:], 1.0 / DH).then_inc(s_pc, 1)
            g.memset(lhs_scale[:], 0.0).then_inc(s_pc, 1)
            g.memset(lhs_shift[:], 0.0).then_inc(s_pc, 1)
            made = [7]

            def select(part, op, fill, base, pattern, row_step):
                pool.wait_ge(s_pc, made[0])
                g.affine_select(out=part, in_=part, compare_op=op, fill=fill, base=base, pattern=pattern,
                                channel_multiplier=row_step).then_inc(s_pc, 1)
                made[0] += 1

            for m in (ident, ident_bf):
                select(m[:], ALU.not_equal, 1.0, 0, [[-1, P]], 1)
            for r in (0, CHUNK):
                select(causal1[r:r + CHUNK, :], ALU.is_ge, MASKED, 0, [[1, CHUNK]], -1)
            for r in (0, 64, 96):
                part = head_sel[r:r + 32, :].rearrange("p (h d) -> p h d", h=HEADS)
                select(part, ALU.not_equal, 1.0, 0, [[-1, HEADS], [0, DH]], 1)
                select(lhs_scale[r:r + 32, :], ALU.is_ge, -1.0, -HEADS, [[0, 1]], 1)
                select(lhs_shift[r:r + 32, :], ALU.is_ge, 1.0, HEADS - 1, [[0, 1]], -1)
            blocks = head_mean[:].rearrange("p (h d) -> p h d", h=HPH)
            select(blocks, ALU.is_ge, 0.0, 0, [[-DH, HPH], [0, DH]], 1)
            select(blocks, ALU.is_ge, 0.0, DH - 1, [[DH, HPH], [0, DH]], -1)
            pool.wait_ge(s_pc, POOL_CONSTANTS)
            pool.wait_ge(s_w, 16 * WEIGHT_LOADS)
            pool.wait_ge(s_vc, VECTOR_CONSTANTS)

            def body(i, attn, later):
                j = i - 1
                if attn:
                    need(pool, qsq_ready, 1, i)
                    g.tensor_tensor(q_sq[:, 0, :], q_sq[:, 0, :], q_sq[:, 1, :],
                                    ALU.add).then_inc(qsum_ready, 1)
                    need(pool, gatea_loaded, 16, i)
                    need(pool, attn_ready, 1, j)
                    g.tensor_tensor(w_o_gated[:], w_o[:],
                                    gate_a[:].unsqueeze(1).to_broadcast([P, HALVES, D]),
                                    ALU.mult).then_inc(wo_ready, 1)
                if later:
                    need(pool, gatef_loaded, 16, j)
                    need(pool, fv_ready, 2, j - 1)
                    g.tensor_tensor(w_fv_gated[:], w_fv[:],
                                    gate_f[:].unsqueeze(1).to_broadcast([P, HALVES, D]),
                                    ALU.mult).then_inc(wv_ready, 1)
                    for half in range(HALVES):
                        need(pool, h2T_ready, 2, j, half + 1)
                        g.tensor_tensor(shift_d[:, half, :], h2T[:, half, 1:T + 1], h2T[:, half, 0:T],
                                        ALU.subtract).then_inc(shift_ready, 1)
                    need(pool, relu_ready, 1, j)
                    g.tensor_tensor(act_T[:], act_T[:], act_T[:], ALU.mult).then_inc(act_ready, 1)
                if attn:
                    need(pool, gmin_ready, 1, i)
                    need(pool, gln_ready, 1, i)
                    g.tensor_tensor(g_log[:], g_log[:], g_exp[:], ALU.subtract).then_inc(gsig_ready, 1)
                    need(pool, state_ready, 1, i)
                    need(pool, pv_ready, 4, i - 1)
                    need(pool, gsig_ready, 1, i)
                    for q in (2, 3):
                        if q == 3:
                            need(pool, sdiag_pool, 2, i, 1)
                        rows = slice(32 * q, 32 * q + 32)
                        g.tensor_tensor(
                            state_diag[rows, :, 1:CHUNKS, 32 * q:32 * q + 32],
                            state[rows, :, :, 0:CHUNKS - 1].rearrange("p a e n -> p a n e"),
                            one[rows, :].unsqueeze(1).unsqueeze(1).to_broadcast([32, HALVES, CHUNKS - 1, 32]),
                            ALU.mult).then_inc(sdiag_pool, 1)
                    need(pool, sdiag_pool, 2, i)
                if later:
                    need(pool, rmin_ready, 1, j)
                    need(pool, rln_ready, 1, j)
                    g.tensor_tensor(r_min[:], r_min[:], r_exp, ALU.subtract).then_inc(rsig_ready, 1)
                    need(pool, ffn_ready, 1, j)
                    g.tensor_tensor(ffn[:], ffn[:], x1[:], ALU.add).then_inc(y_ready, 1)

            schedule(pool, body)

        @block.scalar
        def _(act):
            a = nc.scalar
            a.preload_act_table_set("natural_log_exp_and_others")
            act.wait_ge(s_wmod, 32)
            a.activation(c_tmp[:], cT_sb[:], ACT.Exp, scale=-1.0).then_inc(s_c1, 1)
            act.wait_ge(s_vc, VECTOR_CONSTANTS)

            def body(i, attn, later):
                j = i - 1
                if attn:
                    need(act, ln_stat, 8, i)
                    a.activation(rstd[:], ln_mv[:, :, 1], ACT.Ln, bias=eps_ln[:]).then_inc(ln_log, 1)
                    need(act, ln_log, 1, i)
                    a.activation(rstd[:], rstd[:], ACT.Exp, scale=-0.5).then_inc(rstd_ready, 1)
                if later:
                    need(act, pv_ready, 4, j)
                    a.activation(o_sq[:], bank(4, 2), ACT.Square).then_inc(osq_ready, 1)
                    need(act, ms_ready, 1, j)
                    need(act, gsig_ready, 1, j)
                    need(act, rsig_ready, 1, j - 1)
                    a.activation(g_exp[:], bank(2, 2), ACT.Ln, bias=eps_out[:]).then_inc(mslog_ready, 1)
                if attn:
                    need(act, moda_loaded, 16, i)
                    need(act, g_ready, 2, i - 1)
                    for half in range(HALVES):
                        need(act, zT_ready, 2, i, half + 1)
                        a.activation(hT[:, half, :], bank(half), ACT.Identity,
                                     scale=mod_a[:, half:half + 1],
                                     bias=mod_a[:, 2 + half:3 + half]).then_inc(hT_ready, 1)
                if later:
                    need(act, gexpo_ready, 1, j)
                    a.activation(g_log[:], g_log[:], ACT.Exp).then_inc(gfac_ready, 1)
                if attn:
                    need(act, gt_nabs, 1, i)
                    a.activation(gt_b[:], gt_b[:], ACT.Exp).then_inc(gt_exp, 1)
                    need(act, gt_exp, 1, i)
                    a.activation(gt_b[:], gt_b[:], ACT.Ln, bias=one[:]).then_inc(gt_log, 1)
                    need(act, q_ready, 2, i)
                    a.activation(qT[:], bank(0, 2), ACT.Copy).then_inc(qT_ready, 1)
                    a.activation(q_sq[:], bank(0, 2), ACT.Square).then_inc(qsq_ready, 1)
                if later:
                    need(act, ln2_stat, 8, j)
                    a.activation(rstd2[:], ln2_mv[:, :, 1], ACT.Ln, bias=eps_ln[:]).then_inc(ln2_log, 1)
                    need(act, ln2_log, 1, j)
                    a.activation(rstd2[:], rstd2[:], ACT.Exp, scale=-0.5).then_inc(rstd2_ready, 1)
                if attn:
                    need(act, kvlog_sum, 1, i - 1)
                    for t in range(TILES):
                        need(act, v_ready, 2, i, t // 2 + 1)
                        a.activation(sq_junk[:, t, :], bank(4 + t // 2)[:, 0, (t % 2) * D:(t % 2 + 1) * D],
                                     ACT.Square, accum_out=kv_sumsq[:, 0, t:t + 1]).then_inc(vsq_ready, 1)
                    need(act, e_ready, 2, i)
                    need(act, qdec_ready, 1, i - 1)
                    a.activation(decay_T[:], bank(0, 2), ACT.Exp, scale=1.0 / GATE_NORM).then_inc(decayT_ready, 1)
                    need(act, tail_ready, 1, i)
                    a.activation(k_tail[:], bank(6)[:, 0, 0:TILES * HEADS], ACT.Exp,
                                 scale=1.0 / GATE_NORM).then_inc(ktail_ready, 1)
                    for t in range(TILES):
                        need(act, ktok_ready, 2, i, t // 2 + 1)
                        a.activation(sq_junk[:, TILES + t, :], bank(2 + t // 2)[:, 0, (t % 2) * D:(t % 2 + 1) * D],
                                     ACT.Square, accum_out=kv_sumsq[:, 1, t:t + 1]).then_inc(ksq_ready, 1)
                if later:
                    need(act, modf_loaded, 16, j)
                    need(act, xr_ready, 2, j - 1)
                    need(act, xk_ready, 2, j - 1)
                    for half in range(HALVES):
                        need(act, z2T_ready, 2, j, half + 1)
                        a.activation(h2T[:, half, 1:T + 1], bank(6 + half), ACT.Identity,
                                     scale=mod_f[:, half:half + 1],
                                     bias=mod_f[:, 2 + half:3 + half]).then_inc(h2T_ready, 1)
                if attn:
                    need(act, vsq_ready, 4, i)
                    need(act, ksq_ready, 4, i)
                    a.activation(kv_sumsq[:], kv_sumsq[:], ACT.Ln, scale=1.0 / D,
                                 bias=eps_rms[:]).then_inc(kvlog_ready, 1)
                    need(act, kvlog_sum, 1, i)
                    need(act, vpad_ready, 4, i - 1)
                    a.activation(kv_rms8[:], kv_rms[:].unsqueeze(2).to_broadcast([P, TILES, 8]),
                                 ACT.Exp, scale=-0.5).then_inc(kvrms_ready, 1)
                    need(act, decayT_ready, 1, i)
                    need(act, state_ready, 1, i - 1)
                    for half in range(HALVES):
                        a.activation(chunk_decay[:, half, :, 1:CHUNKS],
                                     decay_T[:, half, 2 * CHUNK - 1::CHUNK].unsqueeze(1).to_broadcast(
                                         [P, 32, CHUNKS - 1]), ACT.Copy).then_inc(cdecay_ready, 1)
                if later:
                    need(act, fk_ready, 2, j)
                    need(act, xk_ready, 2, j)
                    need(act, xr_ready, 2, j)
                    a.activation(act_T[:], bank(6, 2), ACT.Relu).then_inc(relu_ready, 1)
                if attn:
                    need(act, gcopy_ready, 1, i)
                    need(act, gexpo_ready, 1, j)
                    a.activation(g_exp[:], g_copy[:], ACT.Abs).then_inc(gabs_ready, 1)
                    need(act, gabs_ready, 1, i)
                    a.activation(g_exp[:], g_exp[:], ACT.Exp, scale=-1.0).then_inc(gexp_ready, 1)
                    need(act, gexp_ready, 1, i)
                    a.activation(g_exp[:], g_exp[:], ACT.Ln, bias=one[:]).then_inc(gln_ready, 1)
                    for t in range(TILES):
                        need(act, arg_ready, 4, i, t + 1)
                        if t == 0:
                            need(act, attn_ready, 1, j)
                        need(act, probs_ready, 4, i, t - 1)
                        a.activation(decay[:, t % 2, :].rearrange("p (b n) -> p b n", b=2), bank(0, 2),
                                     ACT.Exp, scale=1.0 / GATE_NORM).then_inc(decay_ready, 1)
                        if t == 0:
                            need(act, state_ready, 1, i)
                            need(act, pv_ready, 4, i - 1)
                            for q in (0, 1):
                                rows = slice(32 * q, 32 * q + 32)
                                for half in range(HALVES):
                                    a.activation(
                                        state_diag[rows, half, 1:CHUNKS, 32 * q:32 * q + 32],
                                        state[rows, half, :, 0:CHUNKS - 1].rearrange("p e n -> p n e"),
                                        ACT.Copy).then_inc(sdiag_act, 1)
                        if t == 1 and later:
                            need(act, gsig_ready, 1, i)
                            receptance_log(j)
                        if t == 2 and later:
                            receptance(j)
                elif later:
                    receptance_log(j)
                    receptance(j)

            def receptance_log(j):
                need(act, fr_ready, 2, j)
                a.activation(g_exp[:], bank(6, 2), ACT.Abs).then_inc(rabs_ready, 1)
                need(act, rabs_ready, 1, j)
                a.activation(r_exp, r_exp, ACT.Exp, scale=-1.0).then_inc(rexp_ready, 1)
                need(act, rexp_ready, 1, j)
                a.activation(r_exp, r_exp, ACT.Ln, bias=one[:]).then_inc(rln_ready, 1)

            def receptance(j):
                need(act, rsig_ready, 1, j)
                a.activation(r_min[:], r_min[:], ACT.Exp).then_inc(r_ready, 1)

            schedule(act, body)

        @block.tensor
        def _(pe):
            mm = nc.tensor.matmul

            def project(dst, weight, rhsT, cols, done, feature_major=True):
                for k in range(HALVES):
                    last = mm(dst, weight[:, k, cols], rhsT(k), start=(k == 0), stop=(k == HALVES - 1))
                last.then_inc(done, 1)

            def transposes(src, first_bank, done):
                for half in range(HALVES):
                    for t in range(TILES):
                        last = nc.tensor.transpose(bank(first_bank + half)[:, 0, t * P:(t + 1) * P],
                                                   src[:, t, half * P:(half + 1) * P], ident[:])
                    last.then_inc(done, 1)

            pe.wait_ge(s_wmod, 32)
            pe.wait_ge(s_c2, 3)
            for m in range(NM):
                for k in range(HALVES):
                    mm(bank(0)[:, 0, m * B:(m + 1) * B], wmod_sb[:, k, m * P:(m + 1) * P], c_silu[:, k, :],
                       start=(k == 0), stop=(k == HALVES - 1))
            for n, part in enumerate((2, 5)):
                for k in range(HALVES):
                    last = mm(bank(1)[0:B, 0, n * D:(n + 1) * D], c_silu[:, k, :],
                              wmod_sb[:, k, part * D:(part + 1) * D], start=(k == 0), stop=(k == HALVES - 1))
            last.then_inc(s_modp, 1)
            pe.wait_ge(s_w, 16 * WEIGHT_LOADS)
            pe.wait_ge(s_pc, POOL_CONSTANTS)
            pe.wait_ge(s_vc, VECTOR_CONSTANTS)
            pe.wait_ge(s_mods, 10)

            def attend(i, t):
                need(pe, probs_ready, 4, i, t + 1)
                if t == 0:
                    need(pe, kvnew_ready, 1, i)
                    need(pe, kdec_ready, 2, i)
                    need(pe, qdec_ready, 1, i)
                    need(pe, sdiag_act, 4, i)
                    need(pe, sdiag_pool, 2, i)
                for half in range(HALVES):
                    for c in range(2):
                        n = 2 * t + c
                        cols = slice(n * CHUNK, (n + 1) * CHUNK)
                        for step in range(3 if n else 2):
                            for q in range(PAIRS):
                                dst = bank(4 + half)[32 * q:32 * q + 32, 0, cols]
                                if step < 2:
                                    h = half * HPH + 2 * q + step
                                    last = mm(dst, v_pad[:, c, t, h, :],
                                              probs[:, t % 2, h * CHUNK:(h + 1) * CHUNK],
                                              start=(step == 0), stop=(step == 1 and n == 0))
                                else:
                                    last = mm(dst, state_diag[:, half, n, 32 * q:32 * q + 32],
                                              q_dec[:, half, cols], start=False, stop=True)
                last.then_inc(pv_ready, 1)

            def body(i, attn, later):
                j = i - 1
                if later:
                    need(pe, qsum_ready, 1, j)
                    need(pe, probs_ready, 4, j)
                    for half in range(HALVES):
                        mm(bank(2 + half)[:, 0, :], eps_mean[:], q_sq[:, 0, :], start=True, stop=False,
                           skip_group_check=True)
                    need(pe, osq_ready, 1, j)
                    for half in range(HALVES):
                        last = mm(bank(2 + half)[:, 0, :], head_mean[:], o_sq[:, half, :], start=False,
                                  stop=True, skip_group_check=True)
                    last.then_inc(ms_ready, 1)
                if attn:
                    need(pe, z_ready, 4, i)
                    need(pe, decay_ready, 4, i - 1)
                    transposes(z, 0, zT_ready)
                    need(pe, hT_ready, 2, i)
                    need(pe, ffn_ready, 1, j - 1)
                    for k in range(HALVES):
                        last = mm(bank(6)[:, 0, :], w_gt[:, k, :, :].rearrange("p r h -> p (r h)"), hT[:, k, :],
                                  start=(k == 0), stop=(k == HALVES - 1))
                    last.then_inc(gt_ready, 1)
                    for half in range(HALVES):
                        project(bank(half)[:, 0, :], w_q, lambda k: hT[:, k, :],
                                slice(half * P, half * P + P), q_ready)
                if later:
                    need(pe, og_ready, 1, j)
                    need(pe, wo_ready, 1, j)
                    need(pe, mslog_ready, 1, j)
                    for t in range(TILES):
                        for k in range(HALVES):
                            last = mm(bank(2 + t // 2)[:, 0, (t % 2) * D:(t % 2 + 1) * D],
                                      o_gated[:, k, t * P:(t + 1) * P], w_o_gated[:, k, :],
                                      start=(k == 0), stop=(k == HALVES - 1))
                    last.then_inc(attn_ready, 1)
                if attn:
                    for half in range(HALVES):
                        if half == 1:
                            need(pe, gt_nabs, 1, i)
                        project(bank(7 - half)[:, 0, :], w_k, lambda k: hT[:, k, :],
                                slice(half * P, half * P + P), k_ready)
                    need(pe, ohalf_ready, 1, j)
                    for t in range(TILES):
                        for k in range(HALVES):
                            last = mm(bank(4 + t // 2)[:, 0, (t % 2) * D:(t % 2 + 1) * D],
                                      hT[:, k, t * P:(t + 1) * P], w_v[:, k, :],
                                      start=(k == 0), stop=(k == HALVES - 1))
                        if t % 2:
                            last.then_inc(v_ready, 1)
                    need(pe, split_step, 5, i)
                    need(pe, qT_ready, 1, i)
                    need(pe, qsq_ready, 1, i)
                    for half in range(HALVES):
                        mm(bank(half)[:, 0, :], head_sel[:, half * P:(half + 1) * P], split[:],
                           start=True, stop=True).then_inc(e_ready, 1)
                    need(pe, chunk_end_ready, 1, i)
                    need(pe, kT_ready, 2, i)
                    for t in range(TILES):
                        cols = slice(t * P, (t + 1) * P)
                        dst = bank(6)[:, 0, t * HEADS:(t + 1) * HEADS]
                        mm(dst, split[:, cols], head_sel_neg[:], start=True, stop=False)
                        last = mm(dst, chunk_end[:, cols], head_sel[:, ::DH], start=False, stop=True)
                    last.then_inc(tail_ready, 1)
                    need(pe, x1_ready, 1, j)
                    for t in range(TILES):
                        for half in range(HALVES):
                            last = nc.tensor.transpose(
                                bank(2 + t // 2)[:, 0, (t % 2) * D + half * P:(t % 2) * D + half * P + P],
                                kT[:, half, t * P:(t + 1) * P], ident[:])
                        if t % 2:
                            last.then_inc(ktok_ready, 1)
                if later:
                    need(pe, z2_ready, 4, j)
                    need(pe, ffn_ready, 1, j - 1)
                    if attn:
                        need(pe, ktail_ready, 1, i)
                    transposes(z2, 6, z2T_ready)
                if attn:
                    need(pe, decayT_ready, 1, i)
                    for half in range(HALVES):
                        project(bank(half)[:, 0, :], w_g, lambda k: hT[:, k, :],
                                slice(half * P, half * P + P), g_ready)
                if later:
                    need(pe, xk_ready, 2, j)
                    for half in range(HALVES):
                        project(bank(6 + half)[:, 0, :], w_fk, lambda k: xkT[:, k, :],
                                slice(half * P, half * P + P), fk_ready)
                    need(pe, xr_ready, 2, j)
                    need(pe, relu_ready, 1, j)
                    for t in range(TILES):
                        for k in range(HALVES):
                            last = mm(bank(6 + t // 2)[:, 0, (t % 2) * D:(t % 2 + 1) * D],
                                      xrT[:, k, t * P:(t + 1) * P], w_r[:, k, :],
                                      start=(k == 0), stop=(k == HALVES - 1))
                        if t % 2:
                            last.then_inc(fr_ready, 1)
                if attn:
                    need(pe, vpad_ready, 4, i)
                    need(pe, kdec_ready, 2, i)
                    for half in range(HALVES):
                        for t in range(TILES):
                            for c in range(2):
                                for q in range(PAIRS):
                                    rows = slice(32 * q, 32 * q + 32)
                                    n = half * CHUNKS + 2 * t + c
                                    h = half * HPH + 2 * q
                                    v = v_pad[:, c, t, h:h + 2, :].rearrange("p h e -> p (h e)")
                                    rhs = pair_values(v)
                                    last = mm(bank(4)[rows, 0, n * 32:n * 32 + 32],
                                              k_dec[:, t, half * P + 32 * q:half * P + 32 * q + 32], rhs,
                                              start=True, stop=True)
                    last.then_inc(kv_ready, 1)
                    for t in range(TILES):
                        need(pe, lhs_ready, 1, i)
                        need(pe, rhs_placed, 16 * HEADS, i)
                        if t == 0:
                            need(pe, gcopy_ready, 1, i)
                        else:
                            need(pe, decay_ready, 4, i, t)
                        for half in range(HALVES):
                            mm(bank(half)[:, 0, :], ident_bf[:], causal[:].rearrange("p h n -> p (h n)"),
                               start=True, stop=False, skip_group_check=True)
                            for c in range(2):
                                cols = slice((2 * t + c) * CHUNK, (2 * t + c + 1) * CHUNK)
                                last = mm(bank(half)[CHUNK * c:CHUNK * (c + 1), 0, :].rearrange(
                                              "p (h n) -> p h n", h=HPH),
                                          arg_lhs[:, cols],
                                          arg_rhs[:, half * HPH:(half + 1) * HPH, cols],
                                          start=False, stop=True, skip_group_check=True)
                        last.then_inc(arg_ready, 1)
                        if t == 0:
                            need(pe, q_placed, 16 * HPH, i)
                            need(pe, kdec_ready, 2, i)
                        else:
                            need(pe, probs_ready, 4, i, t)
                        for half in range(HALVES):
                            for c in range(2):
                                cols = slice((2 * t + c) * CHUNK, (2 * t + c + 1) * CHUNK)
                                last = mm(bank(2 + half)[CHUNK * c:CHUNK * (c + 1), 0, :].rearrange(
                                              "p (h n) -> p h n", h=HPH),
                                          kT[:, half, cols], q_diag[:, half, :, cols],
                                          start=True, stop=True)
                        last.then_inc(qk_ready, 1)
                        if t >= 1:
                            attend(i, t - 1)
                        if t == 2 and later:
                            ffn_value(j)
                    attend(i, TILES - 1)
                elif later:
                    ffn_value(j)

            def ffn_value(j):
                need(pe, act_ready, 1, j)
                need(pe, wv_ready, 1, j)
                need(pe, rmin_ready, 1, j)
                for t in range(TILES):
                    for k in range(HALVES):
                        last = mm(bank(6 + t // 2)[:, 0, (t % 2) * D:(t % 2 + 1) * D],
                                  act_T[:, k, t * P:(t + 1) * P], w_fv_gated[:, k, :],
                                  start=(k == 0), stop=(k == HALVES - 1))
                    if t % 2:
                        last.then_inc(fv_ready, 1)

            schedule(pe, body)

        @block.vector
        def _(dve):
            v = nc.vector
            v.memset(eps_ln[:], LN_EPS).then_inc(s_vc, 1)
            v.memset(eps_rms[:], RMS_EPS).then_inc(s_vc, 1)
            v.memset(eps_out[:], RMS_EPS * RMS_EPS * DH).then_inc(s_vc, 1)
            v.memset(eps_mean[:], RMS_EPS * DH / D).then_inc(s_vc, 1)
            v.memset(one[:], 1.0).then_inc(s_vc, 1)
            v.memset(chunk_keep[:], 1.0).then_inc(s_vc, 1)
            v.memset(h2T[:, :, 0:1], 0.0).then_inc(s_vc, 1)
            v.memset(chunk_decay[:], 0.0).then_inc(s_vc, 1)
            v.memset(v_pad[:], 0.0).then_inc(s_vc, 1)
            v.memset(state_diag[:], 0.0).then_inc(s_vc, 1)
            dve.wait_ge(s_vc, 10)
            v.memset(chunk_keep[:, ::CHUNK], 0.0).then_inc(s_vc, 1)
            dve.wait_ge(s_c1, 1)
            v.tensor_scalar(c_tmp[:], c_tmp[:], 1.0, None, ALU.add).then_inc(s_c2, 1)
            dve.wait_ge(s_c2, 1)
            v.reciprocal(c_tmp[:], c_tmp[:]).then_inc(s_c2, 1)
            dve.wait_ge(s_c2, 2)
            dve.wait_ge(s_wmod, 32)
            v.tensor_tensor(c_silu[:], c_tmp[:], cT_sb[:], ALU.mult).then_inc(s_c2, 1)
            dve.wait_ge(s_modp, 1)
            for n, (part, plus) in enumerate(((1, 1.0), (0, 0.0), (4, 1.0), (3, 0.0))):
                v.tensor_scalar(mod_all[:, :, 2 * n:2 * n + 2],
                                bank(0)[:, 0, part * 2 * B:(part + 1) * 2 * B].rearrange("p (m b) -> p b m", m=2),
                                plus, None, ALU.add).then_inc(s_mods, 1)
            rows = bank(1)[0:B, 0, :]
            v.tensor_scalar(gate_tmp, rows, -1.0, None, ALU.mult).then_inc(s_mods, 1)
            dve.wait_ge(s_mods, 5)
            v.tensor_tensor(gate_tmp, gate_tmp, rows, ALU.max).then_inc(s_mods, 1)
            v.tensor_scalar(gate_rows, rows, 0.0, 2.0, ALU.is_ge, ALU.mult).then_inc(s_mods, 1)
            dve.wait_ge(s_mods, 7)
            v.tensor_scalar(gate_rows, gate_rows, -1.0, None, ALU.add).then_inc(s_mods, 1)
            v.tensor_scalar(gate_tmp, gate_tmp, MIN_GATE, None, ALU.max).then_inc(s_mods, 1)
            dve.wait_ge(s_mods, 9)
            v.tensor_tensor(gate_rows, gate_rows, gate_tmp, ALU.mult).then_inc(s_mods, 1)
            dve.wait_ge(s_pc, POOL_CONSTANTS)
            dve.wait_ge(s_w, 16 * WEIGHT_LOADS)
            v.tensor_copy(causal[:], causal1[:].unsqueeze(1).to_broadcast([P, HPH, CHUNK])).then_inc(s_vc, 1)
            v.tensor_scalar(head_sel_neg[:], head_sel[:, ::DH], -1.0, None, ALU.mult).then_inc(s_vc, 1)
            v.tensor_copy(arg_rhs[:], head_sel[:, ::DH].unsqueeze(2).to_broadcast([P, HEADS, T])).then_inc(s_vc, 1)
            for q in range(PAIRS):
                r = slice(32 * q, 32 * q + 32)
                v.tensor_scalar(head_block[r, :], head_mean[r, r], float(DH), None, ALU.mult).then_inc(s_vc, 1)
            v.tensor_copy(w_gt[:], w_gt16[:].unsqueeze(2).to_broadcast([P, HALVES, 8, HEADS])).then_inc(s_vc, 1)
            v.memset(q_diag[:], 0.0).then_inc(s_vc, 1)
            dve.wait_ge(s_vc, VECTOR_CONSTANTS)
            dve.wait_ge(s_modw, 32)

            def norm_stats(i, src, stats, mv, stat_sem):
                for t in range(TILES):
                    v.bn_stats(stats[:, t, :], src[:, t, :]).then_inc(stat_sem, 1)
                need(dve, stat_sem, 8, i, TILES)
                v.memset(carrier[:], 0.0)
                for t in range(TILES):
                    v.bn_aggr(mv[:, t, :], stats[:, t, :]).then_inc(stat_sem, 1)

            def norm_apply(i, src, mv, rstd_sem, rstd_t, dst, dst_sem):
                need(dve, rstd_sem, 1, i)
                for t in range(TILES):
                    v.tensor_scalar(dst[:, t, :], src[:, t, :], mv[:, t, 0:1], rstd_t[:, t:t + 1],
                                    ALU.subtract, ALU.mult).then_inc(dst_sem, 1)

            def body(i, attn, later):
                j = i - 1
                if attn:
                    need(dve, x_loaded, 16, i)
                    norm_stats(i, x_in, ln_stats, ln_mv, ln_stat)
                    need(dve, zT_ready, 2, i - 1)
                    norm_apply(i, x_in, ln_mv, rstd_ready, rstd, z, z_ready)
                if later:
                    need(dve, osq_ready, 1, j)
                    need(dve, gcopy_ready, 1, j)
                    need(dve, probs_ready, 4, j)
                    v.tensor_tensor(o_gated, bank(4, 2), g_copy[:], ALU.mult).then_inc(ohalf_ready, 1)
                    need(dve, mslog_ready, 1, j)
                    need(dve, gsig_ready, 1, j)
                    v.scalar_tensor_tensor(out=g_log[:], in0=g_exp[:], scalar=-0.5, in1=g_log[:],
                                           op0=ALU.mult, op1=ALU.add).then_inc(gexpo_ready, 1)
                    need(dve, gfac_ready, 1, j)
                    need(dve, ohalf_ready, 1, j)
                    v.tensor_tensor(o_gated, o_gated, g_log[:].rearrange("p a t -> p a t"),
                                    ALU.mult).then_inc(og_ready, 1)
                if attn:
                    need(dve, gt_ready, 1, i)
                    v.tensor_scalar(gt_a[:], bank(6)[:, 0, :], 0.0, None, ALU.min).then_inc(gt_min, 1)
                    need(dve, gt_min, 1, i)
                    v.scalar_tensor_tensor(out=gt_b[:], in0=gt_a[:], scalar=2.0, in1=bank(6)[:, 0, :],
                                           op0=ALU.mult, op1=ALU.subtract).then_inc(gt_nabs, 1)
                    need(dve, gt_log, 1, i)
                    v.tensor_tensor(gt_a[:], gt_a[:], gt_b[:], ALU.subtract).then_inc(gt_diff, 1)
                    need(dve, gt_diff, 1, i)
                    v.tensor_tensor_scan(decay_sum[:], chunk_keep[:], gt_a[:], 0.0, ALU.mult,
                                         ALU.add).then_inc(decay_scanned, 1)
                    need(dve, decay_scanned, 1, i)
                    need(dve, tail_ready, 1, i - 1)
                    need(dve, rhs_placed, 16 * HEADS, i - 1)
                    v.tensor_copy(split[:], decay_sum[:]).then_inc(split_step, 1)
                    need(dve, split_step, 5, i, 1)
                    v.tensor_tensor(decay_sum[64:128, :], decay_sum[64:128, :], split[64:128, :],
                                    ALU.subtract).then_inc(split_step, 1)
                    need(dve, split_step, 5, i, 2)
                    v.tensor_copy(split[64:128, :], decay_sum[64:128, :]).then_inc(split_step, 1)
                    need(dve, split_step, 5, i, 3)
                    v.tensor_tensor(decay_sum[96:128, :], decay_sum[96:128, :], split[96:128, :],
                                    ALU.subtract).then_inc(split_step, 1)
                    need(dve, split_step, 5, i, 4)
                    v.tensor_copy(split[96:128, :], decay_sum[96:128, :]).then_inc(split_step, 1)
                if later:
                    need(dve, attn_ready, 1, j)
                    need(dve, xres_loaded, 16, j)
                    v.tensor_tensor(x1[:].rearrange("p (b t) d -> p b (t d)", b=2), bank(2, 2),
                                    x1[:].rearrange("p (b t) d -> p b (t d)", b=2), ALU.add).then_inc(x1_ready, 1)
                    need(dve, x1_ready, 1, j)
                    norm_stats(j, x1, ln2_stats, ln2_mv, ln2_stat)
                if attn:
                    need(dve, split_step, 5, i, 5)
                    need(dve, arg_ready, 4, i - 1)
                    v.tensor_scalar(arg_lhs[:], split[:], lhs_scale[:], lhs_shift[:], ALU.mult,
                                    ALU.add).then_inc(lhs_ready, 1)
                    v.tensor_copy(chunk_end[:].rearrange("p (n c) -> p n c", c=CHUNK),
                                  split[:, CHUNK - 1::CHUNK].unsqueeze(2).to_broadcast(
                                      [P, CHUNKS, CHUNK])).then_inc(chunk_end_ready, 1)
                    for half in range(HALVES):
                        need(dve, k_ready, 2, i, half + 1)
                        if half == 0:
                            need(dve, qk_ready, 4, i - 1)
                        v.tensor_copy(kT[:, half, :], bank(7 - half)[:, 0, :]).then_inc(kT_ready, 1)
                if later:
                    need(dve, z2T_ready, 2, j - 1)
                    norm_apply(j, x1, ln2_mv, rstd2_ready, rstd2, z2, z2_ready)
                if attn:
                    need(dve, kvlog_ready, 1, i)
                    v.tensor_tensor(kv_rms[:], kv_sumsq[:, 0, :], kv_sumsq[:, 1, :],
                                    ALU.add).then_inc(kvlog_sum, 1)
                if later:
                    token_shift(j, 1, xkT, fk_ready, xk_ready)
                if attn:
                    need(dve, kvrms_ready, 1, i)
                    need(dve, pv_ready, 4, i - 1)
                    for b in range(2):
                        for c in range(2):
                            rows = slice(CHUNK * c, CHUNK * (c + 1))
                            v.tensor_tensor(
                                padded_heads(v_pad[rows, c, 2 * b:2 * b + 2, :, :]),
                                bank(4 + b)[rows, 0, :].rearrange("p (a s e) -> p a s e", s=2, e=DH),
                                kv_rms8[rows, 2 * b:2 * b + 2, :].rearrange("p t a -> p (t a)").unsqueeze(2)
                                .unsqueeze(3).to_broadcast([CHUNK, 16, 2, DH]),
                                ALU.mult).then_inc(vpad_ready, 1)
                if later:
                    token_shift(j, 0, xrT, fr_ready, xr_ready)
                if attn:
                    need(dve, ktail_ready, 1, i)
                    need(dve, ksq_ready, 4, i)
                    need(dve, kv_ready, 1, i - 1)
                    for b in range(2):
                        v.tensor_tensor(
                            k_dec[:, 2 * b:2 * b + 2, :].rearrange("p t (h d) -> p (t h) d", h=HEADS),
                            bank(2 + b)[:, 0, :].rearrange("p (h d) -> p h d", d=DH),
                            k_tail[:, 2 * b * HEADS:(2 * b + 2) * HEADS].unsqueeze(2).to_broadcast(
                                [P, 2 * HEADS, DH]),
                            ALU.mult).then_inc(kdec_ready, 1)
                    need(dve, g_ready, 2, i)
                    need(dve, ohalf_ready, 1, j)
                    v.tensor_copy(g_copy[:], bank(0, 2)).then_inc(gcopy_ready, 1)
                    need(dve, gcopy_ready, 1, i)
                    need(dve, og_ready, 1, j)
                    v.tensor_scalar(g_log[:], g_copy[:], 0.0, None, ALU.min).then_inc(gmin_ready, 1)
                    need(dve, decayT_ready, 1, i)
                    need(dve, q_placed, 16 * HPH, i)
                    v.tensor_tensor(q_dec[:], qT[:], decay_T[:], ALU.mult).then_inc(qdec_ready, 1)
                    need(dve, kv_ready, 1, i)
                    v.tensor_tensor(
                        kv_new[:].rearrange("p a e n -> p a n e"),
                        bank(4)[:, 0, :].rearrange("p (a n e) -> p a n e", a=HALVES, n=CHUNKS),
                        head_block[:].unsqueeze(1).unsqueeze(1).to_broadcast([P, HALVES, CHUNKS, 32]),
                        ALU.mult).then_inc(kvnew_ready, 1)
                    need(dve, kvnew_ready, 1, i)
                    need(dve, cdecay_ready, 2, i)
                    need(dve, sdiag_act, 4, i - 1)
                    need(dve, sdiag_pool, 2, i - 1)
                    v.tensor_tensor_scan(state[:].rearrange("p a e n -> p (a e n)"),
                                         chunk_decay[:].rearrange("p a e n -> p (a e n)"),
                                         kv_new[:].rearrange("p a e n -> p (a e n)"),
                                         0.0, ALU.mult, ALU.add).then_inc(state_ready, 1)
                    for t in range(TILES):
                        need(dve, decay_ready, 4, i, t + 1)
                        need(dve, qk_ready, 4, i, t + 1)
                        need(dve, pv_ready, 4, i, t - 1)
                        v.tensor_tensor(probs[:, t % 2, :].rearrange("p (b n) -> p b n", b=2), bank(2, 2),
                                        decay[:, t % 2, :].rearrange("p (b n) -> p b n", b=2),
                                        ALU.mult).then_inc(probs_ready, 1)
                        if t == 1 and later:
                            receptance_min(j)
                    if later:
                        ffn_product(j)
                elif later:
                    receptance_min(j)
                    ffn_product(j)

            def token_shift(j, which, dst, used, done):
                need(dve, used, 2, j - 1)
                for half in range(HALVES):
                    need(dve, shift_ready, 2, j, half + 1)
                    v.scalar_tensor_tensor(out=dst[:, half, :], in0=shift_d[:, half, :],
                                           scalar=mu[:, which, half:half + 1], in1=h2T[:, half, 0:T],
                                           op0=ALU.mult, op1=ALU.add).then_inc(done, 1)

            def receptance_min(j):
                need(dve, rabs_ready, 1, j)
                need(dve, stored, 16, j - 1)
                v.tensor_scalar(r_min[:].rearrange("p (b t) d -> p b (t d)", b=2), bank(6, 2), 0.0, None,
                                ALU.min).then_inc(rmin_ready, 1)

            def ffn_product(j):
                need(dve, fv_ready, 2, j)
                need(dve, r_ready, 1, j)
                v.tensor_tensor(ffn[:].rearrange("p (b t) d -> p b (t d)", b=2), bank(6, 2),
                                r_min[:].rearrange("p (b t) d -> p b (t d)", b=2),
                                ALU.mult).then_inc(ffn_ready, 1)

            schedule(dve, body)


WEIGHT_LOADS = 11
POOL_CONSTANTS = 22
VECTOR_CONSTANTS = 20


def padded_heads(pad):
    rows = pad.shape[0]
    flat = pad.rearrange("p t (a s) e -> p (t a) (s e)", s=2)
    return bass.AP(tensor=flat.tensor, offset=flat.offset, ap=[list(flat.ap[0]), list(flat.ap[1]), [48, 2], [1, 16]])


def pair_values(pair):
    return bass.AP(tensor=pair.tensor, offset=pair.offset, ap=[list(pair.ap[0]), [48, 2], [1, 16]])


_INS = ["L0_attn_x", "L0_attn_Wq", "L0_attn_Wk", "L0_attn_Wv", "L0_attn_Wg", "L0_attn_Wgt", "L0_attn_Wo",
        "L0_ffn_W_r", "L0_ffn_W_k", "L0_ffn_W_v", "L0_ffn_mu_r", "L0_ffn_mu_k", "L0_c", "L0_wmod"]
_TRANSPOSED = {"L0_ffn_W_r", "L0_ffn_W_k", "L0_ffn_W_v", "L0_c"}


def kernel(**inputs):
    import numpy as np
    import concourse.bacc as bacc
    from concourse.bass_utils import run_bass_kernel_spmd

    nc = bacc.Bacc("TRN2", target_bir_lowering=False, num_devices=1)
    arrays, args = {}, []
    for name in _INS:
        a = np.asarray(inputs[name])
        a = np.ascontiguousarray(a.T if name in _TRANSPOSED else a)
        arrays["in_" + name] = a
        args.append(nc.dram_tensor("in_" + name, a.shape, mybir.dt.from_np(a.dtype), kind="ExternalInput").ap())
    shape = inputs["L0_attn_x"].shape
    out = nc.dram_tensor("out_0", tuple(shape), F32, kind="ExternalOutput").ap()
    adaln_block(nc, *args, out)
    r = run_bass_kernel_spmd(nc, [arrays], core_ids=[0])
    return r.results[0]["out_0"]
```

```python
from contextlib import ExitStack

import concourse.bass as bass
from concourse import mybir

ALU = mybir.AluOpType
ACT = mybir.ActivationFunctionType
F32 = mybir.dt.float32
F32R = mybir.dt.float32r
BF16 = mybir.dt.bfloat16

P = 128
BANK = 512
HEADS = 16
CHUNK = 64
GATE_NORM = 16.0
LN_EPS = 1e-5
RMS_EPS = 1e-6
MIN_GATE = 0.25
MASKED = -1e38


def adaln_block(nc, x, Wq, Wk, Wv, Wg, Wgt, Wo, WrT, WkT, WvT, mu_r, mu_k, cT, wmod, out):
    B, T, D = x.shape
    HALVES = D // P
    TILES = T // P
    CHUNKS = T // CHUNK
    DH = D // HEADS
    HPH = HEADS // HALVES
    PAIRS = P // 32
    assert (HALVES, TILES, DH, T, P // CHUNK) == (2, 4, 16, BANK, 2)

    mod_dram = nc.dram_tensor("mod_scratch", (B, P, 8), F32, kind="Internal").ap()
    gate_dram = nc.dram_tensor("gate_scratch", (B, 2 * D), F32, kind="Internal").ap()
    x_tiles = x.rearrange("b (t p) d -> b p t d", p=P)
    out_tiles = out.rearrange("b (t p) d -> b p t d", p=P)

    with ExitStack() as ctx:
        def sb(name, shape, dt=F32):
            return ctx.enter_context(nc.sbuf_tensor(name, shape, dt))

        def sem(name):
            return ctx.enter_context(nc.semaphore(name))

        w_o, w_r, w_fk, w_fv, w_o_gated, w_fv_gated = (
            sb(n, [P, HALVES, D]) for n in ("w_o", "w_r", "w_fk", "w_fv", "w_o_gated", "w_fv_gated"))
        w_q, w_k, w_g, w_v = (sb(n, [P, 2, HALVES, D], F32R) for n in ("w_q", "w_k", "w_g", "w_v"))
        w_gt16 = sb("w_gt16", [P, HALVES, HEADS])
        w_gt = sb("w_gt", [P, 2, HALVES, 8, HEADS], F32R)
        mu = sb("mu", [P, 2, HALVES])
        ident = sb("ident", [P, P])
        ident_bf = sb("ident_bf", [P, P], BF16)
        causal = sb("causal", [P, HPH, CHUNK], BF16)
        causal1 = sb("causal1", [P, CHUNK], BF16)
        head_sel = sb("head_sel", [P, D], BF16)
        head_sel_neg = sb("head_sel_neg", [P, HEADS], BF16)
        lhs_scale = sb("lhs_scale", [P, 1])
        lhs_shift = sb("lhs_shift", [P, 1])
        head_mean = sb("head_mean", [P, P])
        head_block = sb("head_block", [P, 32])
        eps_mean = sb("eps_mean", [P, P])
        chunk_keep = sb("chunk_keep", [P, T])
        eps_ln = sb("eps_ln", [P, 1])
        eps_rms = sb("eps_rms", [P, 1])
        eps_out = sb("eps_out", [P, 1])
        one = sb("one", [P, 1])
        carrier = sb("carrier", [P, 1])

        x_in = sb("x_in", [P, TILES, D])
        mod_a = sb("mod_a", [P, 4])
        gate_a = sb("gate_a", [P, D])
        ln_stats = sb("ln_stats", [P, TILES, 6])
        ln_mv = sb("ln_mv", [P, TILES, 2])
        rstd = sb("rstd", [P, TILES])
        z = sb("z", [P, TILES, D])
        h_hi = sb("h_hi", [P, HALVES, T], F32R)
        h_lo = sb("h_lo", [P, HALVES, T], F32R)
        qT = sb("qT", [P, HALVES, T])
        q_diag = sb("q_diag", [P, HALVES, HPH, T])
        q_sq = sb("q_sq", [P, T])
        q_dec = qT
        kT = sb("kT", [P, HALVES, T])
        k_dec = sb("k_dec", [P, TILES, D])
        q_sq1 = k_dec[:, 0:2, :].rearrange("p t d -> p (t d)")
        v_pad = sb("v_pad", [P, 2, TILES, HEADS, 32])
        g_copy = sb("g_copy", [P, HALVES, T])
        g_log = sb("g_log", [P, HALVES, T])
        g_exp = sb("g_exp", [P, HALVES, T])
        gt_a = sb("gt_a", [P, T])
        gt_b = sb("gt_b", [P, T])
        chunk_end = sb("chunk_end", [P, T], BF16)
        decay_sum = sb("decay_sum", [P, T])
        split = sb("split", [P, T], BF16)
        arg_lhs = sb("arg_lhs", [P, T], BF16)
        arg_rhs = sb("arg_rhs", [P, HEADS, T], BF16)
        k_tail = sb("k_tail", [P, TILES * HEADS])
        kv_sumsq = sb("kv_sumsq", [P, 2, TILES])
        kv_rms = sb("kv_rms", [P, TILES])
        kv_rms8 = sb("kv_rms8", [P, TILES, 8])
        kv_new = sb("kv_new", [P, HALVES, 32, CHUNKS])
        chunk_decay = sb("chunk_decay", [P, HALVES, 32, CHUNKS])
        state = sb("state", [P, HALVES, 32, CHUNKS])
        state_diag = sb("state_diag", [P, HALVES, CHUNKS, P])
        decay = sb("decay", [P, 2, HEADS * CHUNK])
        probs = sb("probs", [P, 2, HEADS * CHUNK])
        o_sq = qT
        o_gated = decay[:, 0, :].rearrange("p (a t) -> p a t", a=HALVES)
        decay_T = o_gated
        sq_junk = decay[:, 1, :].bitcast(BF16).rearrange("p (t d) -> p t d", d=D)
        x1 = sb("x1", [P, TILES, D])
        ln2_stats = sb("ln2_stats", [P, TILES, 6])
        ln2_mv = sb("ln2_mv", [P, TILES, 2])
        rstd2 = sb("rstd2", [P, TILES])
        z2 = z

        mod_f = sb("mod_f", [P, 4])
        gate_f = sb("gate_f", [P, D])
        h2T = sb("h2T", [P, HALVES, T + 1])
        shift_d = sb("shift_d", [P, HALVES, T])
        act_T = shift_d
        xrT = sb("xrT", [P, HALVES, T])
        xkT = g_exp
        hT = xrT
        r_min = sb("r_min", [P, TILES, D])
        r_exp = g_exp[:, :, :].rearrange("p a (b d) -> p (a b) d", d=D)
        ffn = r_min
        wmod_sb = q_diag[:, :, :, :].rearrange("p a h t -> p (a h t)")[:, 0:HALVES * 6 * D].rearrange(
            "p (k n) -> p k n", k=HALVES)
        cT_sb = sb("cT_sb", [P, HALVES, B])
        c_silu = sb("c_silu", [P, HALVES, B])
        c_tmp = sb("c_tmp", [P, HALVES, B])
        w_staged = decay[:].rearrange("p s n -> p (s n)").rearrange("p (w k d) -> p w k d", w=4, k=HALVES)
        mod_rows = qT[:].rearrange("p a t -> p (a t)")[0:B, 0:4 * D]
        mod_all = k_dec[:].rearrange("p t d -> p (t d)")[:, 0:B * 8].rearrange("p (b k) -> p b k", k=8)
        gate_rows = kT[0:B, 0, 0:2 * D]
        gate_tmp = kT[0:B, 1, 0:2 * D]

        ps = ctx.enter_context(nc.psum_tensor("ps", [P, 8, BANK], F32))

        def bank(n, width=1):
            return ps[:, n:n + width, :]

        s_w = sem("weights_loaded")
        s_wmod = sem("wmod_loaded")
        s_whi = sem("weights_rounded")
        s_wlo = sem("weights_rest")
        s_pc = sem("pool_constants")
        s_vc = sem("vector_constants")
        s_c1 = sem("c_exp_done")
        s_c2 = sem("c_silu_steps")
        s_modp = sem("mod_product_ready")
        s_modr = sem("mod_rows_copied")
        s_modf = sem("mod_transposes_ready")
        s_mods = sem("gate_steps")
        s_modt = sem("mod_transposed")
        s_modw = sem("mod_written")
        s_zero = sem("zeros_laid")
        s_rhs0 = sem("arg_rhs_constants")
        x_loaded = sem("x_loaded")
        moda_loaded = sem("moda_loaded")
        gatea_loaded = sem("gatea_loaded")
        modf_loaded = sem("modf_loaded")
        gatef_loaded = sem("gatef_loaded")
        xres_loaded = sem("xres_loaded")
        stored = sem("stored")
        ln_stat = sem("ln_stat")
        ln_log = sem("ln_log")
        rstd_ready = sem("rstd_ready")
        z_ready = sem("z_ready")
        zT_ready = sem("zT_ready")
        hT_ready = sem("hT_ready")
        hhi_ready = sem("hhi_ready")
        hlo_ready = sem("hlo_ready")
        gt_ready = sem("gt_ready")
        gt_min = sem("gt_min")
        gt_abs = sem("gt_abs")
        gt_exp = sem("gt_exp")
        gt_log = sem("gt_log")
        gt_diff = sem("gt_diff")
        decay_scanned = sem("decay_scanned")
        split_step = sem("split_step")
        lhs_ready = sem("lhs_ready")
        chunk_end_ready = sem("chunk_end_ready")
        rhs_placed = sem("rhs_placed")
        q_ready = sem("q_ready")
        k_ready = sem("k_ready")
        g_ready = sem("g_ready")
        v_ready = sem("v_ready")
        qsq_ready = sem("qsq_ready")
        qT_ready = sem("qT_ready")
        qsum_ready = sem("qsum_ready")
        q_placed = sem("q_placed")
        kT_ready = sem("kT_ready")
        gcopy_ready = sem("gcopy_ready")
        gmin_ready = sem("gmin_ready")
        gabs_ready = sem("gabs_ready")
        gexp_ready = sem("gexp_ready")
        gln_ready = sem("gln_ready")
        gsig_ready = sem("gsig_ready")
        vsq_ready = sem("vsq_ready")
        ktok_ready = sem("ktok_ready")
        ksq_ready = sem("ksq_ready")
        kvlog_ready = sem("kvlog_ready")
        kvlog_sum = sem("kvlog_sum")
        kvrms_ready = sem("kvrms_ready")
        vpad_ready = sem("vpad_ready")
        e_ready = sem("e_ready")
        decayT_ready = sem("decayT_ready")
        tail_ready = sem("tail_ready")
        ktail_ready = sem("ktail_ready")
        kdec_ready = sem("kdec_ready")
        qdec_ready = sem("qdec_ready")
        kv_ready = sem("kv_ready")
        kvnew_ready = sem("kvnew_ready")
        cdecay_ready = sem("cdecay_ready")
        state_ready = sem("state_ready")
        sdiag_act = sem("sdiag_act")
        sdiag_pool = sem("sdiag_pool")
        arg_ready = sem("arg_ready")
        decay_ready = sem("decay_ready")
        qk_ready = sem("qk_ready")
        probs_ready = sem("probs_ready")
        pv_ready = sem("pv_ready")
        osq_ready = sem("osq_ready")
        ms_ready = sem("ms_ready")
        mslog_ready = sem("mslog_ready")
        gexpo_ready = sem("gexpo_ready")
        gfac_ready = sem("gfac_ready")
        ohalf_ready = sem("ohalf_ready")
        og_ready = sem("og_ready")
        wo_ready = sem("wo_ready")
        attn_ready = sem("attn_ready")
        x1_ready = sem("x1_ready")
        ln2_stat = sem("ln2_stat")
        ln2_log = sem("ln2_log")
        rstd2_ready = sem("rstd2_ready")
        z2_ready = sem("z2_ready")
        z2T_ready = sem("z2T_ready")
        h2T_ready = sem("h2T_ready")
        shift_ready = sem("shift_ready")
        shift1_ready = sem("shift1_ready")
        xk0_ready = sem("xk0_ready")
        xk_ready = sem("xk_ready")
        xr_ready = sem("xr_ready")
        fk_ready = sem("fk_ready")
        relu_ready = sem("relu_ready")
        act_ready = sem("act_ready")
        fr_ready = sem("fr_ready")
        rabs_ready = sem("rabs_ready")
        rmin_ready = sem("rmin_ready")
        rexp_ready = sem("rexp_ready")
        rln_ready = sem("rln_ready")
        rsig_ready = sem("rsig_ready")
        r_ready = sem("r_ready")
        wv_ready = sem("wv_ready")
        fv_ready = sem("fv_ready")
        ffn_ready = sem("ffn_ready")
        y_ready = sem("y_ready")

        block = ctx.enter_context(nc.Block())

        def need(eng, s, per, i, k=None):
            value = per * i + (per if k is None else k)
            if isinstance(value, int) and value <= 0:
                return
            eng.wait_ge(s, value)

        def schedule(eng, body):
            body(0, True, False)
            body(1, True, True)
            with eng.Fori(2, B - 1) as i:
                body(i, True, True)
            body(B - 1, True, True, following=False)
            body(B, False, True)


        def element(dram, i):
            return dram[i:i + 1] if isinstance(i, int) else dram[bass.ds(i, 1)]

        def tokens(dram, i):
            return element(dram, i).rearrange("b p t d -> (b p) t d")

        def columns(dram, i, a, b):
            return element(dram, i)[:, :, a:b].rearrange("b p k -> (b p) k")

        def gate_row(i, a, b):
            return element(gate_dram, i)[:, a:b].rearrange("b d -> (b d)").partition_broadcast(P)

        @block.sync
        def _(sp):
            sp.dma_start(cT_sb[:], cT.rearrange("(k p) n -> p k n", p=P)).then_inc(s_wmod, 16)
            sp.dma_start(wmod_sb, wmod.rearrange("(k p) n -> p k n", p=P)).then_inc(s_wmod, 16)
            sp.dma_start(x_in[:], tokens(x_tiles, 0)).then_inc(x_loaded, 16)
            for dst, src in ((w_gt16[:], Wgt), (w_staged[:, 0], Wq), (w_staged[:, 1], Wk), (w_staged[:, 2], Wg),
                             (w_staged[:, 3], Wv), (w_o[:], Wo), (w_r[:], WrT), (w_fk[:], WkT), (w_fv[:], WvT)):
                sp.dma_start(dst, src.rearrange("(k p) n -> p k n", p=P)).then_inc(s_w, 16)
            for n, src in enumerate((mu_r, mu_k)):
                sp.dma_start(mu[:, n, :], src.rearrange("(k p) -> p k", p=P), allow_slow_non_contiguous=True).then_inc(s_w, 16)
            sp.wait_ge(s_mods, 6)
            sp.dma_start(gate_dram, gate_rows).then_inc(s_modw, 16)
            sp.wait_ge(s_modt, 4)
            sp.dma_start(mod_dram.rearrange("b p k -> p b k"), mod_all).then_inc(s_modw, 16)
            sp.wait_ge(s_modw, 32)
            sp.dma_start(gate_a[:], gate_row(0, 0, D)).then_inc(gatea_loaded, 16)
            sp.wait_ge(s_zero, 3)
            sp.wait_ge(s_rhs0, 1)

            def body(i, attn, later, following=True):
                j = i - 1
                if attn:
                    if following:
                        need(sp, z_ready, 4, i)
                        sp.dma_start(x_in[:], tokens(x_tiles, i + 1)).then_inc(x_loaded, 16)
                        need(sp, hT_ready, 2, i)
                        sp.dma_start(mod_a[:], columns(mod_dram, i + 1, 0, 4)).then_inc(moda_loaded, 16)
                    need(sp, qk_ready, 4, i - 1)
                    need(sp, qT_ready, 1, i)
                    for h in range(HPH):
                        rows = slice(DH * h, DH * (h + 1))
                        sp.dma_start(q_diag[rows, :, h, :], qT[rows, :, :]).then_inc(q_placed, 16)
                    need(sp, arg_ready, 4, i - 1)
                    need(sp, split_step, 5, i)
                    for r in PART_ROWS:
                        sp.dma_start(arg_rhs[r + HEADS:r + HEADS + 1, :, :],
                                     split[r:r + HEADS, :]).then_inc(rhs_placed, 16)
                    if following:
                        need(sp, wo_ready, 1, i)
                        sp.dma_start(gate_a[:], gate_row(i + 1, 0, D)).then_inc(gatea_loaded, 16)
                    need(sp, h2T_ready, 2, j)
                    sp.dma_start(mod_f[:], columns(mod_dram, i, 4, 8)).then_inc(modf_loaded, 16)
                    need(sp, wv_ready, 1, j)
                    sp.dma_start(gate_f[:], gate_row(i, D, 2 * D)).then_inc(gatef_loaded, 16)
                if later:
                    need(sp, y_ready, 1, j)
                    sp.dma_start(tokens(out_tiles, j), ffn[:]).then_inc(stored, 16)
                if attn:
                    sp.dma_start(x1[:], tokens(x_tiles, i)).then_inc(xres_loaded, 16)

            schedule(sp, body)
            sp.wait_ge(stored, 16 * B)

        @block.gpsimd
        def _(pool):
            g = nc.gpsimd
            g.memset(ident[:], 0.0).then_inc(s_pc, 1)
            g.memset(ident_bf[:], 0.0).then_inc(s_pc, 1)
            g.memset(causal1[:], 0.0).then_inc(s_pc, 1)
            g.memset(head_sel[:], 0.0).then_inc(s_pc, 1)
            g.memset(head_mean[:], 1.0 / DH).then_inc(s_pc, 1)
            g.memset(lhs_scale[:], 0.0).then_inc(s_pc, 1)
            g.memset(lhs_shift[:], 0.0).then_inc(s_pc, 1)
            made = [7]

            def select(part, op, fill, base, pattern, row_step):
                pool.wait_ge(s_pc, made[0])
                g.affine_select(out=part, in_=part, compare_op=op, fill=fill, base=base, pattern=pattern,
                                channel_multiplier=row_step).then_inc(s_pc, 1)
                made[0] += 1

            for m in (ident, ident_bf):
                select(m[:], ALU.not_equal, 1.0, 0, [[-1, P]], 1)
            for r in (0, CHUNK):
                select(causal1[r:r + CHUNK, :], ALU.is_ge, MASKED, 0, [[1, CHUNK]], -1)
            for r in PART_ROWS:
                part = head_sel[r:r + 32, :].rearrange("p (h d) -> p h d", h=HEADS)
                select(part, ALU.not_equal, 1.0, 0, [[-1, HEADS], [0, DH]], 1)
                select(lhs_scale[r:r + 32, :], ALU.is_ge, -1.0, -HEADS, [[0, 1]], 1)
                select(lhs_shift[r:r + 32, :], ALU.is_ge, 1.0, HEADS - 1, [[0, 1]], -1)
            blocks = head_mean[:].rearrange("p (h d) -> p h d", h=HPH)
            select(blocks, ALU.is_ge, 0.0, 0, [[-DH, HPH], [0, DH]], 1)
            select(blocks, ALU.is_ge, 0.0, DH - 1, [[DH, HPH], [0, DH]], -1)
            pool.wait_ge(s_pc, POOL_CONSTANTS)
            g.memset(v_pad[:], 0.0).then_inc(s_zero, 1)
            g.memset(state_diag[:], 0.0).then_inc(s_zero, 1)
            pool.wait_ge(s_modp, 1)
            g.memset(q_diag[:], 0.0).then_inc(s_zero, 1)
            pool.wait_ge(s_zero, 3)
            pool.wait_ge(s_w, 16 * WEIGHT_LOADS)
            pool.wait_ge(s_vc, VECTOR_CONSTANTS)
            pool.wait_ge(s_modt, 4)

            def body(i, attn, later, following=True):
                j = i - 1
                if attn:
                    need(pool, qT_ready, 1, i)
                    need(pool, ms_ready, 1, j)
                    need(pool, kv_ready, 1, i - 1)
                    g.tensor_tensor(q_sq[:], qT[:, 0, :], qT[:, 0, :], ALU.mult).then_inc(qsq_ready, 1)
                    g.tensor_tensor(q_sq1, qT[:, 1, :], qT[:, 1, :], ALU.mult).then_inc(qsq_ready, 1)
                    need(pool, qsq_ready, 2, i)
                    g.tensor_tensor(q_sq[:], q_sq[:], q_sq1,
                                    ALU.add).then_inc(qsum_ready, 1)
                    need(pool, gatea_loaded, 16, i)
                    need(pool, attn_ready, 1, j)
                    g.tensor_tensor(w_o_gated[:], w_o[:],
                                    gate_a[:].unsqueeze(1).to_broadcast([P, HALVES, D]),
                                    ALU.mult).then_inc(wo_ready, 1)
                if later:
                    need(pool, gatef_loaded, 16, j)
                    need(pool, fv_ready, 2, j - 1)
                    g.tensor_tensor(w_fv_gated[:], w_fv[:],
                                    gate_f[:].unsqueeze(1).to_broadcast([P, HALVES, D]),
                                    ALU.mult).then_inc(wv_ready, 1)
                    need(pool, h2T_ready, 2, j, 1)
                    g.tensor_tensor(shift_d[:, 0, :], h2T[:, 0, 1:T + 1], h2T[:, 0, 0:T],
                                    ALU.subtract).then_inc(shift_ready, 1)
                    need(pool, relu_ready, 2, j)
                    g.tensor_tensor(act_T[:], act_T[:], act_T[:], ALU.mult).then_inc(act_ready, 1)
                if attn:
                    need(pool, gmin_ready, 1, i)
                    need(pool, gln_ready, 1, i)
                    g.tensor_tensor(g_log[:], g_log[:], g_exp[:], ALU.subtract).then_inc(gsig_ready, 1)
                    need(pool, state_ready, 1, i)
                    need(pool, pv_ready, 4, i - 1)
                    need(pool, gsig_ready, 1, i)
                    for q in (2, 3):
                        if q == 3:
                            need(pool, sdiag_pool, 2, i, 1)
                        rows = slice(32 * q, 32 * q + 32)
                        g.tensor_tensor(
                            state_diag[rows, :, 1:CHUNKS, 32 * q:32 * q + 32],
                            state[rows, :, :, 0:CHUNKS - 1].rearrange("p a e n -> p a n e"),
                            one[rows, :].unsqueeze(1).unsqueeze(1).to_broadcast([32, HALVES, CHUNKS - 1, 32]),
                            ALU.mult).then_inc(sdiag_pool, 1)
                    need(pool, sdiag_pool, 2, i)
                if later:
                    need(pool, rmin_ready, 1, j)
                    need(pool, rln_ready, 1, j)
                    g.tensor_tensor(r_min[:], r_min[:], r_exp, ALU.subtract).then_inc(rsig_ready, 1)
                    need(pool, ffn_ready, 1, j)
                    g.tensor_tensor(ffn[:], ffn[:], x1[:], ALU.add).then_inc(y_ready, 1)

            schedule(pool, body)

        @block.scalar
        def _(act):
            a = nc.scalar
            a.preload_act_table_set("natural_log_exp_and_others")
            act.wait_ge(s_wmod, 32)
            a.activation(c_tmp[:], cT_sb[:], ACT.Exp, scale=-1.0).then_inc(s_c1, 1)

            def body(i, attn, later, following=True):
                j = i - 1
                if later:
                    need(act, pv_ready, 4, j)
                    a.activation(o_sq[:], bank(4, 2), ACT.Square).then_inc(osq_ready, 1)
                if attn:
                    need(act, moda_loaded, 16, i)
                    need(act, g_ready, 2, i - 1)
                    need(act, fr_ready, 2, j - 1)
                    for half in range(HALVES):
                        need(act, zT_ready, 2, i, half + 1)
                        a.activation(hT[:, half, :], bank(half), ACT.Identity,
                                     scale=mod_a[:, half:half + 1],
                                     bias=mod_a[:, 2 + half:3 + half]).then_inc(hT_ready, 1)
                        need(act, hT_ready, 2, i, half + 1)
                        a.activation(h_hi[:, half, :], hT[:, half, :], ACT.Copy).then_inc(hhi_ready, 1)
                if later:
                    need(act, ms_ready, 1, j)
                    need(act, gsig_ready, 1, j)
                    need(act, rsig_ready, 1, j - 1)
                    a.activation(g_exp[:], bank(2, 2), ACT.Ln, bias=eps_out[:]).then_inc(mslog_ready, 1)
                    need(act, gexpo_ready, 1, j)
                    a.activation(g_log[:], g_log[:], ACT.Exp).then_inc(gfac_ready, 1)
                if attn:
                    need(act, gt_ready, 1, i)
                    need(act, gt_diff, 1, j)
                    a.activation(gt_b[:], bank(6)[:, 0, :], ACT.Abs).then_inc(gt_abs, 1)
                    need(act, gt_abs, 1, i)
                    a.activation(gt_b[:], gt_b[:], ACT.Exp, scale=-1.0).then_inc(gt_exp, 1)
                    need(act, gt_exp, 1, i)
                    a.activation(gt_b[:], gt_b[:], ACT.Ln, bias=one[:]).then_inc(gt_log, 1)
                    need(act, q_ready, 2, i)
                    a.activation(qT[:], bank(0, 2), ACT.Copy).then_inc(qT_ready, 1)
                    need(act, qk_ready, 4, i - 1)
                    copy_k(i, 0)
                    need(act, split_step, 5, i)
                    need(act, tail_ready, 1, i - 1)
                    a.activation(chunk_end[:].rearrange("p (n c) -> p n c", c=CHUNK),
                                 split[:, CHUNK - 1::CHUNK].unsqueeze(2).to_broadcast([P, CHUNKS, CHUNK]),
                                 ACT.Copy).then_inc(chunk_end_ready, 1)
                    copy_k(i, 1)
                if later:
                    need(act, ln2_stat, 8, j)
                    a.activation(rstd2[:], ln2_mv[:, :, 1], ACT.Ln, bias=eps_ln[:]).then_inc(ln2_log, 1)
                    need(act, ln2_log, 1, j)
                    a.activation(rstd2[:], rstd2[:], ACT.Exp, scale=-0.5).then_inc(rstd2_ready, 1)
                if attn:
                    need(act, kvlog_sum, 1, i - 1)
                    for t in range(TILES):
                        need(act, v_ready, 2, i, t // 2 + 1)
                        a.activation(sq_junk[:, t, :], bank(4 + t // 2)[:, 0, (t % 2) * D:(t % 2 + 1) * D],
                                     ACT.Square, accum_out=kv_sumsq[:, 0, t:t + 1]).then_inc(vsq_ready, 1)
                    need(act, tail_ready, 1, i)
                    a.activation(k_tail[:], bank(7)[:, 0, 0:TILES * HEADS], ACT.Exp,
                                 scale=1.0 / GATE_NORM).then_inc(ktail_ready, 1)
                    need(act, e_ready, 2, i)
                    need(act, attn_ready, 1, j)
                    a.activation(decay_T, bank(0, 2), ACT.Exp, scale=1.0 / GATE_NORM).then_inc(decayT_ready, 1)
                if later:
                    second_modulated(j, 0)
                    second_modulated(j, 1)
                if attn:
                    for t in range(TILES):
                        need(act, ktok_ready, 2, i, t // 2 + 1)
                        a.activation(sq_junk[:, TILES + t, :], bank(2 + t // 2)[:, 0, (t % 2) * D:(t % 2 + 1) * D],
                                     ACT.Square, accum_out=kv_sumsq[:, 1, t:t + 1]).then_inc(ksq_ready, 1)
                if attn:
                    need(act, vsq_ready, 4, i)
                    need(act, ksq_ready, 4, i)
                    a.activation(kv_sumsq[:], kv_sumsq[:], ACT.Ln, scale=1.0 / D,
                                 bias=eps_rms[:]).then_inc(kvlog_ready, 1)
                    need(act, kvlog_sum, 1, i)
                    need(act, vpad_ready, 4, i - 1)
                    a.activation(kv_rms8[:], kv_rms[:].unsqueeze(2).to_broadcast([P, TILES, 8]),
                                 ACT.Exp, scale=-0.5).then_inc(kvrms_ready, 1)
                    need(act, decayT_ready, 1, i)
                    need(act, state_ready, 1, i - 1)
                    for half in range(HALVES):
                        a.activation(chunk_decay[:, half, :, 1:CHUNKS],
                                     decay_T[:, half, 2 * CHUNK - 1::CHUNK].unsqueeze(1).to_broadcast(
                                         [P, 32, CHUNKS - 1]), ACT.Copy).then_inc(cdecay_ready, 1)
                if later:
                    need(act, xk_ready, 2, j)
                    need(act, xr_ready, 2, j)
                    for half in range(HALVES):
                        need(act, fk_ready, 2, j, half + 1)
                        a.activation(act_T[:, half, :], bank(6 + half)[:, 0, :],
                                     ACT.Relu).then_inc(relu_ready, 1)
                if attn:
                    need(act, gcopy_ready, 1, i)
                    need(act, gexpo_ready, 1, j)
                    a.activation(g_exp[:], g_copy[:], ACT.Abs).then_inc(gabs_ready, 1)
                    need(act, gabs_ready, 1, i)
                    a.activation(g_exp[:], g_exp[:], ACT.Exp, scale=-1.0).then_inc(gexp_ready, 1)
                    need(act, gexp_ready, 1, i)
                    a.activation(g_exp[:], g_exp[:], ACT.Ln, bias=one[:]).then_inc(gln_ready, 1)
                    for t in range(TILES):
                        need(act, arg_ready, 4, i, t + 1)
                        if t == 0:
                            need(act, qdec_ready, 1, i)
                        need(act, probs_ready, 4, i, t - 1)
                        a.activation(decay[:, t % 2, :].rearrange("p (b n) -> p b n", b=2), bank(0, 2),
                                     ACT.Exp, scale=1.0 / GATE_NORM).then_inc(decay_ready, 1)
                        if t == 0:
                            need(act, state_ready, 1, i)
                            need(act, pv_ready, 4, i - 1)
                            for q in (0, 1):
                                rows = slice(32 * q, 32 * q + 32)
                                for half in range(HALVES):
                                    a.activation(
                                        state_diag[rows, half, 1:CHUNKS, 32 * q:32 * q + 32],
                                        state[rows, half, :, 0:CHUNKS - 1].rearrange("p e n -> p n e"),
                                        ACT.Copy).then_inc(sdiag_act, 1)
                        if t == 1 and later:
                            need(act, gsig_ready, 1, i)
                            receptance_log(j)
                        if t == 2 and following:
                            first_rstd(i + 1)
                        if t == 2 and later:
                            receptance(j)
                elif later:
                    receptance_log(j)
                    receptance(j)

            def copy_k(i, half):
                need(act, k_ready, 2, i, half + 1)
                a.activation(kT[:, half, :], bank(half)[:, 0, :], ACT.Copy).then_inc(kT_ready, 1)

            def second_modulated(j, half):
                need(act, modf_loaded, 16, j)
                need(act, xr_ready, 2, j - 1)
                need(act, xk_ready, 2, j - 1)
                need(act, z2T_ready, 2, j, half + 1)
                a.activation(h2T[:, half, 1:T + 1], bank(6 + half), ACT.Identity,
                             scale=mod_f[:, half:half + 1],
                             bias=mod_f[:, 2 + half:3 + half]).then_inc(h2T_ready, 1)

            def first_rstd(i):
                need(act, ln_stat, 8, i)
                a.activation(rstd[:], ln_mv[:, :, 1], ACT.Ln, bias=eps_ln[:]).then_inc(ln_log, 1)
                need(act, ln_log, 1, i)
                a.activation(rstd[:], rstd[:], ACT.Exp, scale=-0.5).then_inc(rstd_ready, 1)

            def receptance_log(j):
                need(act, fr_ready, 2, j)
                a.activation(g_exp[:], bank(6, 2), ACT.Abs).then_inc(rabs_ready, 1)
                need(act, rabs_ready, 1, j)
                a.activation(r_exp, r_exp, ACT.Exp, scale=-1.0).then_inc(rexp_ready, 1)
                need(act, rexp_ready, 1, j)
                a.activation(r_exp, r_exp, ACT.Ln, bias=one[:]).then_inc(rln_ready, 1)

            def receptance(j):
                need(act, rsig_ready, 1, j)
                a.activation(r_min[:], r_min[:], ACT.Exp).then_inc(r_ready, 1)

            first_rstd(0)
            act.wait_ge(s_w, 16 * WEIGHT_LOADS)
            for n, w in enumerate((w_q, w_k, w_g, w_v)):
                a.activation(w[:, 0], w_staged[:, n], ACT.Copy).then_inc(s_whi, 1)
            act.wait_ge(s_modp, 1)
            for n in range(2):
                a.activation(mod_rows[:, n * 2 * D:(n + 1) * 2 * D], bank(6 + n)[0:B, 0, :],
                             ACT.Copy).then_inc(s_modr, 1)
            act.wait_ge(s_pc, POOL_CONSTANTS)
            a.activation(arg_rhs[:], head_sel[:, ::DH].unsqueeze(2).to_broadcast([P, HEADS, T]),
                         ACT.Copy).then_inc(s_rhs0, 1)
            act.wait_ge(s_vc, VECTOR_CONSTANTS)
            act.wait_ge(s_wlo, 4)
            act.wait_ge(s_modw, 32)
            schedule(act, body)

        @block.tensor
        def _(pe):
            mm = nc.tensor.matmul

            def project(dst, weight, rhsT, cols, done):
                for k in range(HALVES):
                    last = mm(dst, weight[:, k, cols], rhsT[:, k, :], start=(k == 0), stop=(k == HALVES - 1))
                last.then_inc(done, 1)

            def split_passes():
                passes = [(w, x, k) for w, x in ((0, h_hi), (1, h_hi), (0, h_lo)) for k in range(HALVES)]
                return [(n == 0, n == len(passes) - 1) + p for n, p in enumerate(passes)]

            def project_h(dst, weight, done):
                for first, final, w, x, k in split_passes():
                    last = mm(dst, weight(w, k), x[:, k, :], start=first, stop=final)
                last.then_inc(done, 1)

            def transposes(src, first_bank, done):
                for half in range(HALVES):
                    for t in range(TILES):
                        last = nc.tensor.transpose(bank(first_bank + half)[:, 0, t * P:(t + 1) * P],
                                                   src[:, t, half * P:(half + 1) * P], ident[:])
                    last.then_inc(done, 1)

            pe.wait_ge(s_wmod, 32)
            pe.wait_ge(s_c2, 3)
            for dst, cols in ((bank(6)[0:B, 0, :], 0), (bank(7)[0:B, 0, :], 3 * D),
                              (bank(0)[0:B, 0, 0:D], 2 * D), (bank(0)[0:B, 0, D:2 * D], 5 * D)):
                width = dst.shape[-1]
                for k in range(HALVES):
                    last = mm(dst, c_silu[:, k, :], wmod_sb[:, k, cols:cols + width],
                              start=(k == 0), stop=(k == HALVES - 1))
            last.then_inc(s_modp, 1)
            pe.wait_ge(s_pc, POOL_CONSTANTS)
            pe.wait_ge(s_modr, 2)
            for m in range(8):
                last = nc.tensor.transpose(bank(1)[:, 0, m * B:(m + 1) * B], mod_rows[:, m * P:(m + 1) * P],
                                           ident[0:B, 0:B])
            last.then_inc(s_modf, 1)
            pe.wait_ge(s_w, 16 * WEIGHT_LOADS)
            pe.wait_ge(s_vc, VECTOR_CONSTANTS)
            pe.wait_ge(s_mods, 6)
            pe.wait_ge(s_modt, 4)
            pe.wait_ge(s_wlo, 4)

            def attend(i, t):
                need(pe, probs_ready, 4, i, t + 1)
                if t == 0:
                    need(pe, kvnew_ready, 1, i)
                    need(pe, kdec_ready, 2, i)
                    need(pe, qdec_ready, 1, i)
                    need(pe, sdiag_act, 4, i)
                    need(pe, sdiag_pool, 2, i)
                for half in range(HALVES):
                    for c in range(2):
                        n = 2 * t + c
                        cols = slice(n * CHUNK, (n + 1) * CHUNK)
                        for step in range(3 if n else 2):
                            for q in range(PAIRS):
                                dst = bank(4 + half)[32 * q:32 * q + 32, 0, cols]
                                if step < 2:
                                    h = half * HPH + 2 * q + step
                                    last = mm(dst, v_pad[:, c, t, h, :],
                                              probs[:, t % 2, h * CHUNK:(h + 1) * CHUNK],
                                              start=(step == 0), stop=(step == 1 and n == 0))
                                else:
                                    last = mm(dst, state_diag[:, half, n, 32 * q:32 * q + 32],
                                              q_dec[:, half, cols], start=False, stop=True)
                last.then_inc(pv_ready, 1)

            def body(i, attn, later, following=True):
                j = i - 1
                if attn:
                    need(pe, z_ready, 4, i)
                    need(pe, decay_ready, 4, i - 1)
                    transposes(z, 0, zT_ready)
                if later:
                    need(pe, qsum_ready, 1, j)
                    need(pe, probs_ready, 4, j)
                    for half in range(HALVES):
                        mm(bank(2 + half)[:, 0, :], eps_mean[:], q_sq[:], start=True, stop=False,
                           skip_group_check=True)
                    need(pe, osq_ready, 1, j)
                    for half in range(HALVES):
                        last = mm(bank(2 + half)[:, 0, :], head_mean[:], o_sq[:, half, :], start=False,
                                  stop=True, skip_group_check=True)
                    last.then_inc(ms_ready, 1)
                if attn:
                    need(pe, hhi_ready, 2, i)
                    need(pe, ffn_ready, 1, j - 1)
                    for first, final, w, h, k in split_passes():
                        if h is h_lo:
                            need(pe, hlo_ready, 2, i, k + 1)
                        last = mm(bank(6)[:, 0, :], w_gt[:, w, k].rearrange("p r h -> p (r h)"), h[:, k, :],
                                  start=first, stop=final)
                    last.then_inc(gt_ready, 1)
                    for half in range(HALVES):
                        project_h(bank(half)[:, 0, :],
                                  lambda w, k: w_q[:, w, k, half * P:half * P + P], q_ready)
                if later:
                    need(pe, og_ready, 1, j)
                    need(pe, wo_ready, 1, j)
                    need(pe, mslog_ready, 1, j)
                    for t in range(TILES):
                        for k in range(HALVES):
                            last = mm(bank(2 + t // 2)[:, 0, (t % 2) * D:(t % 2 + 1) * D],
                                      o_gated[:, k, t * P:(t + 1) * P], w_o_gated[:, k, :],
                                      start=(k == 0), stop=(k == HALVES - 1))
                    last.then_inc(attn_ready, 1)
                if attn:
                    need(pe, qT_ready, 1, i)
                    for half in range(HALVES):
                        project_h(bank(half)[:, 0, :],
                                  lambda w, k: w_k[:, w, k, half * P:half * P + P], k_ready)
                    need(pe, ohalf_ready, 1, j)
                    for t in range(TILES):
                        for first, final, w, h, k in split_passes():
                            last = mm(bank(4 + t // 2)[:, 0, (t % 2) * D:(t % 2 + 1) * D],
                                      h[:, k, t * P:(t + 1) * P], w_v[:, w, k, :], start=first, stop=final)
                        if t % 2:
                            last.then_inc(v_ready, 1)
                    need(pe, chunk_end_ready, 1, i)
                    need(pe, split_step, 5, i)
                    for t in range(TILES):
                        cols = slice(t * P, (t + 1) * P)
                        dst = bank(7)[:, 0, t * HEADS:(t + 1) * HEADS]
                        mm(dst, split[:, cols], head_sel_neg[:], start=True, stop=False)
                        last = mm(dst, chunk_end[:, cols], head_sel[:, ::DH], start=False, stop=True)
                    last.then_inc(tail_ready, 1)
                    need(pe, kT_ready, 2, i)
                    for half in range(HALVES):
                        mm(bank(half)[:, 0, :], head_sel[:, half * P:(half + 1) * P], split[:],
                           start=True, stop=True).then_inc(e_ready, 1)
                    need(pe, x1_ready, 1, j)
                    for t in range(TILES):
                        for half in range(HALVES):
                            last = nc.tensor.transpose(
                                bank(2 + t // 2)[:, 0, (t % 2) * D + half * P:(t % 2) * D + half * P + P],
                                kT[:, half, t * P:(t + 1) * P], ident[:])
                        if t % 2:
                            last.then_inc(ktok_ready, 1)
                if later:
                    need(pe, z2_ready, 4, j)
                    if attn:
                        need(pe, ktail_ready, 1, i)
                        need(pe, gt_min, 1, i)
                    else:
                        need(pe, ffn_ready, 1, j - 1)
                    transposes(z2, 6, z2T_ready)
                if attn:
                    need(pe, decayT_ready, 1, i)
                    for half in range(HALVES):
                        project_h(bank(half)[:, 0, :],
                                  lambda w, k: w_g[:, w, k, half * P:half * P + P], g_ready)
                if later:
                    need(pe, xk_ready, 2, j)
                    for half in range(HALVES):
                        project(bank(6 + half)[:, 0, :], w_fk, xkT,
                                slice(half * P, half * P + P), fk_ready)
                    receptance_logits(j, 0)
                    if not attn:
                        receptance_logits(j, 1)
                if attn:
                    need(pe, vpad_ready, 4, i)
                    need(pe, kdec_ready, 2, i)
                    for half in range(HALVES):
                        for t in range(TILES):
                            for c in range(2):
                                for q in range(PAIRS):
                                    rows = slice(32 * q, 32 * q + 32)
                                    n = half * CHUNKS + 2 * t + c
                                    h = half * HPH + 2 * q
                                    v = v_pad[:, c, t, h:h + 2, :].rearrange("p h e -> p (h e)")
                                    rhs = pair_values(v)
                                    last = mm(bank(4)[rows, 0, n * 32:n * 32 + 32],
                                              k_dec[:, t, half * P + 32 * q:half * P + 32 * q + 32], rhs,
                                              start=True, stop=True)
                    last.then_inc(kv_ready, 1)
                    for t in range(TILES):
                        need(pe, lhs_ready, 1, i)
                        need(pe, rhs_placed, 16 * len(PART_ROWS), i)
                        if t == 0:
                            need(pe, gcopy_ready, 1, i)
                        else:
                            need(pe, decay_ready, 4, i, t)
                        for half in range(HALVES):
                            mm(bank(half)[:, 0, :], ident_bf[:], causal[:].rearrange("p h n -> p (h n)"),
                               start=True, stop=False, skip_group_check=True)
                            for c in range(2):
                                cols = slice((2 * t + c) * CHUNK, (2 * t + c + 1) * CHUNK)
                                last = mm(bank(half)[CHUNK * c:CHUNK * (c + 1), 0, :].rearrange(
                                              "p (h n) -> p h n", h=HPH),
                                          arg_lhs[:, cols],
                                          arg_rhs[:, half * HPH:(half + 1) * HPH, cols],
                                          start=False, stop=True, skip_group_check=True)
                        last.then_inc(arg_ready, 1)
                        if t == 1 and later:
                            receptance_logits(j, 1)
                        if t == 0:
                            need(pe, q_placed, 16 * HPH, i)
                            need(pe, kdec_ready, 2, i)
                        else:
                            need(pe, probs_ready, 4, i, t)
                        for half in range(HALVES):
                            for c in range(2):
                                cols = slice((2 * t + c) * CHUNK, (2 * t + c + 1) * CHUNK)
                                last = mm(bank(2 + half)[CHUNK * c:CHUNK * (c + 1), 0, :].rearrange(
                                              "p (h n) -> p h n", h=HPH),
                                          kT[:, half, cols], q_diag[:, half, :, cols],
                                          start=True, stop=True)
                        last.then_inc(qk_ready, 1)
                        if t >= 1:
                            attend(i, t - 1)
                        if t == 2 and later:
                            ffn_value(j)
                    attend(i, TILES - 1)
                elif later:
                    ffn_value(j)

            def receptance_logits(j, pair):
                need(pe, xr_ready, 2, j)
                need(pe, relu_ready, 2, j, pair + 1)
                for t in (2 * pair, 2 * pair + 1):
                    for k in range(HALVES):
                        last = mm(bank(6 + pair)[:, 0, (t % 2) * D:(t % 2 + 1) * D],
                                  xrT[:, k, t * P:(t + 1) * P], w_r[:, k, :],
                                  start=(k == 0), stop=(k == HALVES - 1))
                last.then_inc(fr_ready, 1)

            def ffn_value(j):
                need(pe, act_ready, 1, j)
                need(pe, wv_ready, 1, j)
                need(pe, rmin_ready, 1, j)
                for t in range(TILES):
                    for k in range(HALVES):
                        last = mm(bank(6 + t // 2)[:, 0, (t % 2) * D:(t % 2 + 1) * D],
                                  act_T[:, k, t * P:(t + 1) * P], w_fv_gated[:, k, :],
                                  start=(k == 0), stop=(k == HALVES - 1))
                    if t % 2:
                        last.then_inc(fv_ready, 1)

            schedule(pe, body)

        @block.vector
        def _(dve):
            v = nc.vector
            v.memset(eps_ln[:], LN_EPS).then_inc(s_vc, 1)
            v.memset(eps_rms[:], RMS_EPS).then_inc(s_vc, 1)
            v.memset(eps_out[:], RMS_EPS * RMS_EPS * DH).then_inc(s_vc, 1)
            v.memset(eps_mean[:], RMS_EPS * DH / D).then_inc(s_vc, 1)
            v.memset(one[:], 1.0).then_inc(s_vc, 1)
            v.memset(chunk_keep[:], 1.0).then_inc(s_vc, 1)
            v.memset(h2T[:, :, 0:1], 0.0).then_inc(s_vc, 1)
            v.memset(chunk_decay[:], 0.0).then_inc(s_vc, 1)
            dve.wait_ge(s_vc, 8)
            v.memset(chunk_keep[:, ::CHUNK], 0.0).then_inc(s_vc, 1)
            dve.wait_ge(s_c1, 1)
            v.tensor_scalar(c_tmp[:], c_tmp[:], 1.0, None, ALU.add).then_inc(s_c2, 1)
            dve.wait_ge(s_c2, 1)
            v.reciprocal(c_tmp[:], c_tmp[:]).then_inc(s_c2, 1)
            dve.wait_ge(s_c2, 2)
            dve.wait_ge(s_wmod, 32)
            v.tensor_tensor(c_silu[:], c_tmp[:], cT_sb[:], ALU.mult).then_inc(s_c2, 1)
            dve.wait_ge(s_pc, POOL_CONSTANTS)
            v.tensor_copy(causal[:], causal1[:].unsqueeze(1).to_broadcast([P, HPH, CHUNK])).then_inc(s_vc, 1)
            v.tensor_scalar(head_sel_neg[:], head_sel[:, ::DH], -1.0, None, ALU.mult).then_inc(s_vc, 1)
            for q in range(PAIRS):
                r = slice(32 * q, 32 * q + 32)
                v.tensor_scalar(head_block[r, :], head_mean[r, r], float(DH), None, ALU.mult).then_inc(s_vc, 1)

            def modulation():
                dve.wait_ge(s_modf, 1)
                for n, (part, plus) in enumerate(((1, 1.0), (0, 0.0), (3, 1.0), (2, 0.0))):
                    v.tensor_scalar(mod_all[:, :, 2 * n:2 * n + 2],
                                    bank(1)[:, 0, part * 2 * B:(part + 1) * 2 * B].rearrange("p (m b) -> p b m", m=2),
                                    plus, None, ALU.add).then_inc(s_modt, 1)
                dve.wait_ge(s_modt, 4)
                v.tensor_copy(mod_a[:], mod_all[:, 0, 0:4]).then_inc(moda_loaded, 16)
                rows = bank(0)[0:B, 0, :]
                v.tensor_scalar(gate_tmp, rows, -1.0, None, ALU.mult).then_inc(s_mods, 1)
                dve.wait_ge(s_mods, 1)
                v.tensor_tensor(gate_tmp, gate_tmp, rows, ALU.max).then_inc(s_mods, 1)
                v.tensor_scalar(gate_rows, rows, 0.0, 2.0, ALU.is_ge, ALU.mult).then_inc(s_mods, 1)
                dve.wait_ge(s_mods, 3)
                v.tensor_scalar(gate_rows, gate_rows, -1.0, None, ALU.add).then_inc(s_mods, 1)
                v.tensor_scalar(gate_tmp, gate_tmp, MIN_GATE, None, ALU.max).then_inc(s_mods, 1)
                dve.wait_ge(s_mods, 5)
                v.tensor_tensor(gate_rows, gate_rows, gate_tmp, ALU.mult).then_inc(s_mods, 1)

            def norm_stats(i, src, stats, mv, stat_sem):
                for t in range(TILES):
                    v.bn_stats(stats[:, t, :], src[:, t, :]).then_inc(stat_sem, 1)
                need(dve, stat_sem, 8, i, TILES)
                v.memset(carrier[:], 0.0)
                for t in range(TILES):
                    v.bn_aggr(mv[:, t, :], stats[:, t, :]).then_inc(stat_sem, 1)

            def norm_apply(i, src, mv, rstd_sem, rstd_t, dst, dst_sem):
                need(dve, rstd_sem, 1, i)
                for t in range(TILES):
                    v.tensor_scalar(dst[:, t, :], src[:, t, :], mv[:, t, 0:1], rstd_t[:, t:t + 1],
                                    ALU.subtract, ALU.mult).then_inc(dst_sem, 1)

            def body(i, attn, later, following=True):
                j = i - 1
                if later:
                    need(dve, osq_ready, 1, j)
                    need(dve, gcopy_ready, 1, j)
                    need(dve, probs_ready, 4, j)
                    v.tensor_tensor(o_gated, bank(4, 2), g_copy[:], ALU.mult).then_inc(ohalf_ready, 1)
                if attn:
                    need(dve, g_ready, 2, i - 1)
                    for half in range(HALVES):
                        need(dve, hhi_ready, 2, i, half + 1)
                        v.tensor_tensor(h_lo[:, half, :], hT[:, half, :], h_hi[:, half, :],
                                        ALU.subtract).then_inc(hlo_ready, 1)
                if later:
                    need(dve, mslog_ready, 1, j)
                    need(dve, gsig_ready, 1, j)
                    v.scalar_tensor_tensor(out=g_log[:], in0=g_exp[:], scalar=-0.5, in1=g_log[:],
                                           op0=ALU.mult, op1=ALU.add).then_inc(gexpo_ready, 1)
                    need(dve, gfac_ready, 1, j)
                    need(dve, ohalf_ready, 1, j)
                    v.tensor_tensor(o_gated, o_gated, g_log[:].rearrange("p a t -> p a t"),
                                    ALU.mult).then_inc(og_ready, 1)
                if attn:
                    need(dve, gt_abs, 1, i)
                    v.tensor_scalar(gt_a[:], bank(6)[:, 0, :], 0.0, None, ALU.min).then_inc(gt_min, 1)
                    need(dve, gt_min, 1, i)
                    need(dve, gt_log, 1, i)
                    v.tensor_tensor(gt_a[:], gt_a[:], gt_b[:], ALU.subtract).then_inc(gt_diff, 1)
                    need(dve, gt_diff, 1, i)
                    v.tensor_tensor_scan(decay_sum[:], chunk_keep[:], gt_a[:], 0.0, ALU.mult,
                                         ALU.add).then_inc(decay_scanned, 1)
                    need(dve, decay_scanned, 1, i)
                    need(dve, tail_ready, 1, i - 1)
                    need(dve, rhs_placed, 16 * len(PART_ROWS), i - 1)
                    v.tensor_copy(split[:], decay_sum[:]).then_inc(split_step, 1)
                    need(dve, split_step, 5, i, 1)
                    v.tensor_tensor(decay_sum[64:128, :], decay_sum[64:128, :], split[64:128, :],
                                    ALU.subtract).then_inc(split_step, 1)
                    need(dve, split_step, 5, i, 2)
                    v.tensor_copy(split[64:128, :], decay_sum[64:128, :]).then_inc(split_step, 1)
                    need(dve, split_step, 5, i, 3)
                    v.tensor_tensor(decay_sum[96:128, :], decay_sum[96:128, :], split[96:128, :],
                                    ALU.subtract).then_inc(split_step, 1)
                    need(dve, split_step, 5, i, 4)
                    v.tensor_copy(split[96:128, :], decay_sum[96:128, :]).then_inc(split_step, 1)
                if later:
                    need(dve, attn_ready, 1, j)
                    need(dve, xres_loaded, 16, j)
                    v.tensor_tensor(x1[:].rearrange("p (b t) d -> p b (t d)", b=2), bank(2, 2),
                                    x1[:].rearrange("p (b t) d -> p b (t d)", b=2), ALU.add).then_inc(x1_ready, 1)
                    need(dve, x1_ready, 1, j)
                    norm_stats(j, x1, ln2_stats, ln2_mv, ln2_stat)
                if later:
                    need(dve, z2T_ready, 2, j - 1)
                    if attn:
                        need(dve, zT_ready, 2, i)
                    norm_apply(j, x1, ln2_mv, rstd2_ready, rstd2, z2, z2_ready)
                if attn:
                    need(dve, split_step, 5, i)
                    need(dve, arg_ready, 4, i - 1)
                    v.tensor_scalar(arg_lhs[:], split[:], lhs_scale[:], lhs_shift[:], ALU.mult,
                                    ALU.add).then_inc(lhs_ready, 1)
                if later:
                    need(dve, h2T_ready, 2, j)
                    need(dve, fv_ready, 2, j - 1)
                    v.tensor_tensor(shift_d[:, 1, :], h2T[:, 1, 1:T + 1], h2T[:, 1, 0:T],
                                    ALU.subtract).then_inc(shift1_ready, 1)
                    token_shift(j, 1, xkT, fk_ready, xk_ready)
                    token_shift(j, 0, xrT, fr_ready, xr_ready)
                if attn:
                    need(dve, kvlog_ready, 1, i)
                    v.tensor_tensor(kv_rms[:], kv_sumsq[:, 0, :], kv_sumsq[:, 1, :],
                                    ALU.add).then_inc(kvlog_sum, 1)
                    need(dve, kvrms_ready, 1, i)
                    need(dve, pv_ready, 4, i - 1)
                    for b in range(2):
                        for c in range(2):
                            rows = slice(CHUNK * c, CHUNK * (c + 1))
                            v.tensor_tensor(
                                padded_heads(v_pad[rows, c, 2 * b:2 * b + 2, :, :]),
                                bank(4 + b)[rows, 0, :].rearrange("p (a s e) -> p a s e", s=2, e=DH),
                                kv_rms8[rows, 2 * b:2 * b + 2, :].rearrange("p t a -> p (t a)").unsqueeze(2)
                                .unsqueeze(3).to_broadcast([CHUNK, 16, 2, DH]),
                                ALU.mult).then_inc(vpad_ready, 1)
                    need(dve, ktail_ready, 1, i)
                    need(dve, ksq_ready, 4, i)
                    need(dve, kv_ready, 1, i - 1)
                    need(dve, qsum_ready, 1, i)
                    for b in range(2):
                        v.tensor_tensor(
                            k_dec[:, 2 * b:2 * b + 2, :].rearrange("p t (h d) -> p (t h) d", h=HEADS),
                            bank(2 + b)[:, 0, :].rearrange("p (h d) -> p h d", d=DH),
                            k_tail[:, 2 * b * HEADS:(2 * b + 2) * HEADS].unsqueeze(2).to_broadcast(
                                [P, 2 * HEADS, DH]),
                            ALU.mult).then_inc(kdec_ready, 1)
                    need(dve, g_ready, 2, i)
                    need(dve, ohalf_ready, 1, j)
                    v.tensor_copy(g_copy[:], bank(0, 2)).then_inc(gcopy_ready, 1)
                    need(dve, gcopy_ready, 1, i)
                    need(dve, og_ready, 1, j)
                    v.tensor_scalar(g_log[:], g_copy[:], 0.0, None, ALU.min).then_inc(gmin_ready, 1)
                    need(dve, decayT_ready, 1, i)
                    need(dve, q_placed, 16 * HPH, i)
                    need(dve, qsq_ready, 2, i)
                    v.tensor_tensor(q_dec[:], qT[:], decay_T, ALU.mult).then_inc(qdec_ready, 1)
                    need(dve, kv_ready, 1, i)
                    v.tensor_tensor(
                        kv_new[:].rearrange("p a e n -> p a n e"),
                        bank(4)[:, 0, :].rearrange("p (a n e) -> p a n e", a=HALVES, n=CHUNKS),
                        head_block[:].unsqueeze(1).unsqueeze(1).to_broadcast([P, HALVES, CHUNKS, 32]),
                        ALU.mult).then_inc(kvnew_ready, 1)
                    need(dve, kvnew_ready, 1, i)
                    need(dve, cdecay_ready, 2, i)
                    need(dve, sdiag_act, 4, i - 1)
                    need(dve, sdiag_pool, 2, i - 1)
                    v.tensor_tensor_scan(state[:].rearrange("p a e n -> p (a e n)"),
                                         chunk_decay[:].rearrange("p a e n -> p (a e n)"),
                                         kv_new[:].rearrange("p a e n -> p (a e n)"),
                                         0.0, ALU.mult, ALU.add).then_inc(state_ready, 1)
                    for t in range(TILES):
                        need(dve, decay_ready, 4, i, t + 1)
                        need(dve, qk_ready, 4, i, t + 1)
                        need(dve, pv_ready, 4, i, t - 1)
                        v.tensor_tensor(probs[:, t % 2, :].rearrange("p (b n) -> p b n", b=2), bank(2, 2),
                                        decay[:, t % 2, :].rearrange("p (b n) -> p b n", b=2),
                                        ALU.mult).then_inc(probs_ready, 1)
                        if t == 1 and later:
                            receptance_min(j)
                        if t == 2 and following:
                            first_norm(i + 1, later)
                    if later:
                        ffn_product(j)
                elif later:
                    receptance_min(j)
                    ffn_product(j)

            def first_norm(i, later):
                need(dve, x_loaded, 16, i)
                norm_stats(i, x_in, ln_stats, ln_mv, ln_stat)
                need(dve, zT_ready, 2, i - 1)
                if later:
                    need(dve, z2T_ready, 2, i - 2)
                norm_apply(i, x_in, ln_mv, rstd_ready, rstd, z, z_ready)

            def token_shift(j, which, dst, used, done):
                need(dve, used, 2, j - 1)
                for half, shifted in ((1, shift1_ready), (0, shift_ready)):
                    need(dve, shifted, 1, j)
                    v.scalar_tensor_tensor(out=dst[:, half, :], in0=shift_d[:, half, :],
                                           scalar=mu[:, which, half:half + 1], in1=h2T[:, half, 0:T],
                                           op0=ALU.mult, op1=ALU.add).then_inc(done, 1)

            def receptance_min(j):
                need(dve, rabs_ready, 1, j)
                need(dve, stored, 16, j - 1)
                v.tensor_scalar(r_min[:].rearrange("p (b t) d -> p b (t d)", b=2), bank(6, 2), 0.0, None,
                                ALU.min).then_inc(rmin_ready, 1)

            def ffn_product(j):
                need(dve, fv_ready, 2, j)
                need(dve, r_ready, 1, j)
                v.tensor_tensor(ffn[:].rearrange("p (b t) d -> p b (t d)", b=2), bank(6, 2),
                                r_min[:].rearrange("p (b t) d -> p b (t d)", b=2),
                                ALU.mult).then_inc(ffn_ready, 1)

            first_norm(0, False)
            dve.wait_ge(s_w, 16 * WEIGHT_LOADS)
            v.tensor_copy(w_gt[:, 0], w_gt16[:].unsqueeze(2).to_broadcast([P, HALVES, 8, HEADS])).then_inc(s_vc, 1)
            dve.wait_ge(s_vc, VECTOR_CONSTANTS - 1)
            v.tensor_tensor(w_gt[:, 1], w_gt16[:].unsqueeze(2).to_broadcast([P, HALVES, 8, HEADS]), w_gt[:, 0],
                            ALU.subtract).then_inc(s_vc, 1)
            for n, w in enumerate((w_q, w_k, w_g, w_v)):
                dve.wait_ge(s_whi, n + 1)
                v.tensor_tensor(w[:, 1], w_staged[:, n], w[:, 0], ALU.subtract).then_inc(s_wlo, 1)
            dve.wait_ge(s_vc, VECTOR_CONSTANTS)
            modulation()
            dve.wait_ge(s_zero, 3)
            dve.wait_ge(s_modw, 32)
            schedule(dve, body)


PART_ROWS = (0, 64, 96)
WEIGHT_LOADS = 11
POOL_CONSTANTS = 22
VECTOR_CONSTANTS = 17


def padded_heads(pad):
    rows = pad.shape[0]
    flat = pad.rearrange("p t (a s) e -> p (t a) (s e)", s=2)
    return bass.AP(tensor=flat.tensor, offset=flat.offset, ap=[list(flat.ap[0]), list(flat.ap[1]), [48, 2], [1, 16]])


def pair_values(pair):
    return bass.AP(tensor=pair.tensor, offset=pair.offset, ap=[list(pair.ap[0]), [48, 2], [1, 16]])


_INS = ["L0_attn_x", "L0_attn_Wq", "L0_attn_Wk", "L0_attn_Wv", "L0_attn_Wg", "L0_attn_Wgt", "L0_attn_Wo",
        "L0_ffn_W_r", "L0_ffn_W_k", "L0_ffn_W_v", "L0_ffn_mu_r", "L0_ffn_mu_k", "L0_c", "L0_wmod"]
_TRANSPOSED = {"L0_ffn_W_r", "L0_ffn_W_k", "L0_ffn_W_v", "L0_c"}


def kernel(**inputs):
    import numpy as np
    import concourse.bacc as bacc
    from concourse.bass_utils import run_bass_kernel_spmd

    nc = bacc.Bacc("TRN2", target_bir_lowering=False, num_devices=1)
    arrays, args = {}, []
    for name in _INS:
        a = np.asarray(inputs[name])
        a = np.ascontiguousarray(a.T if name in _TRANSPOSED else a)
        arrays["in_" + name] = a
        args.append(nc.dram_tensor("in_" + name, a.shape, mybir.dt.from_np(a.dtype), kind="ExternalInput").ap())
    shape = inputs["L0_attn_x"].shape
    out = nc.dram_tensor("out_0", tuple(shape), F32, kind="ExternalOutput").ap()
    adaln_block(nc, *args, out)
    r = run_bass_kernel_spmd(nc, [arrays], core_ids=[0])
    return r.results[0]["out_0"]
```

```python
from contextlib import ExitStack

import concourse.bass as bass
from concourse import mybir

ALU = mybir.AluOpType
ACT = mybir.ActivationFunctionType
F32 = mybir.dt.float32
F32R = mybir.dt.float32r
BF16 = mybir.dt.bfloat16

P = 128
BANK = 512
HEADS = 16
CHUNK = 64
GATE_NORM = 16.0
LN_EPS = 1e-5
RMS_EPS = 1e-6
MIN_GATE = 0.25
MASKED = -1e38


def adaln_block(nc, x, Wq, Wk, Wv, Wg, Wgt, Wo, WrT, WkT, WvT, mu_r, mu_k, cT, wmod, out):
    B, T, D = x.shape
    HALVES = D // P
    TILES = T // P
    CHUNKS = T // CHUNK
    DH = D // HEADS
    HPH = HEADS // HALVES
    PAIRS = P // 32
    EPS_MEAN = RMS_EPS * DH / D
    assert (HALVES, TILES, DH, T, P // CHUNK) == (2, 4, 16, BANK, 2)

    mod_dram = nc.dram_tensor("mod_scratch", (B, P, 8), F32, kind="Internal").ap()
    gate_dram = nc.dram_tensor("gate_scratch", (B, 2 * D), F32, kind="Internal").ap()
    x_tiles = x.rearrange("b (t p) d -> b p t d", p=P)
    out_tiles = out.rearrange("b (t p) d -> b p t d", p=P)

    with ExitStack() as ctx:
        def sb(name, shape, dt=F32):
            return ctx.enter_context(nc.sbuf_tensor(name, shape, dt))

        def sem(name):
            return ctx.enter_context(nc.semaphore(name))

        w_o, w_r, w_fk, w_fv, w_o_gated, w_fv_gated = (
            sb(n, [P, HALVES, D]) for n in ("w_o", "w_r", "w_fk", "w_fv", "w_o_gated", "w_fv_gated"))
        w_q, w_k, w_g, w_v = (sb(n, [P, 2, HALVES, D], F32R) for n in ("w_q", "w_k", "w_g", "w_v"))
        w_gt16 = sb("w_gt16", [P, HALVES, HEADS])
        w_gt = sb("w_gt", [P, 2, HALVES, 8, HEADS], F32R)
        mu = sb("mu", [P, 2, HALVES])
        ident = sb("ident", [P, P])
        mask_lhs1 = sb("mask_lhs1", [P, CHUNK], BF16)
        mask_rhs1 = sb("mask_rhs1", [P, CHUNK], BF16)
        lhs_const = sb("lhs_const", [P, T], BF16)
        head_sel = sb("head_sel", [P, D], BF16)
        head_sel_neg = sb("head_sel_neg", [P, HEADS], BF16)
        lhs_scale = sb("lhs_scale", [P, 1])
        head_mean = sb("head_mean", [P, P])
        head_block = sb("head_block", [P, 32])
        ones = sb("ones", [P, P], F32R)
        chunk_keep = sb("chunk_keep", [P, T])
        eps_ln = sb("eps_ln", [P, 1])
        eps_rms = sb("eps_rms", [P, 1])
        eps_out = sb("eps_out", [P, 1])
        one = sb("one", [P, 1])
        carrier = sb("carrier", [P, 1])

        x_in = sb("x_in", [P, TILES, D])
        mod_a = sb("mod_a", [P, 4])
        gate_a = sb("gate_a", [P, D])
        ln_stats = sb("ln_stats", [P, TILES, 6])
        ln_mv = sb("ln_mv", [P, TILES, 2])
        rstd = sb("rstd", [P, TILES])
        z = sb("z", [P, TILES, D])
        h_hi = sb("h_hi", [P, HALVES, T], F32R)
        h_lo = sb("h_lo", [P, HALVES, T], F32R)
        qT = sb("qT", [P, HALVES, T])
        q_diag = sb("q_diag", [P, HALVES, HPH, T])
        q_eps = sb("q_eps", [P, 2, T], F32R)
        q_dec = qT
        kT = sb("kT", [P, HALVES, T])
        k_dec = sb("k_dec", [P, TILES, D])
        q_sq = k_dec[:, 2:4, :].rearrange("p t d -> p (t d)")
        q_sq1 = k_dec[:, 0:2, :].rearrange("p t d -> p (t d)")
        v_pad = sb("v_pad", [P, 2, TILES, HEADS, 32])
        g_copy = sb("g_copy", [P, HALVES, T])
        g_log = sb("g_log", [P, HALVES, T])
        g_exp = sb("g_exp", [P, HALVES, T])
        gt_a = sb("gt_a", [P, T])
        gt_b = sb("gt_b", [P, T])
        kv_new = gt_b[:].rearrange("p (a e n) -> p a e n", a=HALVES, n=CHUNKS)
        chunk_end = sb("chunk_end", [P, T], BF16)
        decay_sum = sb("decay_sum", [P, T])
        split = sb("split", [P, T], BF16)
        arg_lhs = sb("arg_lhs", [P, T], BF16)
        arg_rhs = sb("arg_rhs", [P, HEADS, T], BF16)
        k_tail = sb("k_tail", [P, TILES * HEADS])
        kv_sumsq = sb("kv_sumsq", [P, 2, TILES])
        kv_rms = sb("kv_rms", [P, TILES])
        kv_rms8 = sb("kv_rms8", [P, TILES, 8])
        chunk_decay = sb("chunk_decay", [P, HALVES, 32, CHUNKS])
        state = sb("state", [P, HALVES, 32, CHUNKS])
        state_diag = sb("state_diag", [P, HALVES, CHUNKS, P])
        decay = sb("decay", [P, 2, HEADS * CHUNK])
        probs = sb("probs", [P, 2, HEADS * CHUNK])
        o_sq = qT
        o_gated = decay[:, 0, :].rearrange("p (a t) -> p a t", a=HALVES)
        decay_T = o_gated
        sq_junk = decay[:, 1, :].bitcast(BF16).rearrange("p (t d) -> p t d", d=D)
        x1 = sb("x1", [P, TILES, D])
        ln2_stats = sb("ln2_stats", [P, TILES, 6])
        ln2_mv = sb("ln2_mv", [P, TILES, 2])
        rstd2 = sb("rstd2", [P, TILES])
        z2 = z

        mod_f = sb("mod_f", [P, 4])
        gate_f = sb("gate_f", [P, D])
        h2T = sb("h2T", [P, HALVES, T + 1])
        shift_d = sb("shift_d", [P, HALVES, T])
        act_T = shift_d
        xrT = sb("xrT", [P, HALVES, T])
        xkT = g_exp
        hT = xrT
        r_min = sb("r_min", [P, TILES, D])
        r_exp = g_exp[:, :, :].rearrange("p a (b d) -> p (a b) d", d=D)
        ffn = r_min
        wmod_sb = q_diag[:, :, :, :].rearrange("p a h t -> p (a h t)")[:, 0:HALVES * 6 * D].rearrange(
            "p (k n) -> p k n", k=HALVES)
        cT_sb = sb("cT_sb", [P, HALVES, B])
        c_silu = sb("c_silu", [P, HALVES, B])
        c_tmp = sb("c_tmp", [P, HALVES, B])
        w_staged = decay[:].rearrange("p s n -> p (s n)").rearrange("p (w k d) -> p w k d", w=4, k=HALVES)
        mod_rows = qT[:].rearrange("p a t -> p (a t)")[0:B, 0:4 * D]
        mod_all = k_dec[:].rearrange("p t d -> p (t d)")[:, 0:B * 8].rearrange("p (b k) -> p b k", k=8)
        gate_rows = g_exp[0:B, 0, 0:2 * D]
        gate_tmp = g_exp[0:B, 1, 0:2 * D]

        ps = ctx.enter_context(nc.psum_tensor("ps", [P, 8, BANK], F32))

        def bank(n, width=1):
            return ps[:, n:n + width, :]

        s_w = sem("weights_loaded")
        s_wmod = sem("wmod_loaded")
        s_whi = sem("weights_rounded")
        s_wlo = sem("weights_rest")
        s_pc = sem("pool_constants")
        s_vc = sem("vector_constants")
        s_c1 = sem("c_exp_done")
        s_c2 = sem("c_silu_steps")
        s_modp = sem("mod_product_ready")
        s_modr = sem("mod_rows_copied")
        s_modf = sem("mod_transposes_ready")
        s_mods = sem("gate_steps")
        s_modt = sem("mod_transposed")
        s_modw = sem("mod_written")
        s_zero = sem("zeros_laid")
        s_rhs0 = sem("arg_rhs_constants")
        x_loaded = sem("x_loaded")
        moda_loaded = sem("moda_loaded")
        gatea_loaded = sem("gatea_loaded")
        modf_loaded = sem("modf_loaded")
        gatef_loaded = sem("gatef_loaded")
        xres_loaded = sem("xres_loaded")
        stored = sem("stored")
        ln_stat = sem("ln_stat")
        ln_log = sem("ln_log")
        rstd_ready = sem("rstd_ready")
        z_ready = sem("z_ready")
        zT_ready = sem("zT_ready")
        hT_ready = sem("hT_ready")
        hhi_ready = sem("hhi_ready")
        hlo_ready = sem("hlo_ready")
        gt_ready = sem("gt_ready")
        gt_min = sem("gt_min")
        gt_abs = sem("gt_abs")
        gt_exp = sem("gt_exp")
        gt_log = sem("gt_log")
        gt_diff = sem("gt_diff")
        decay_scanned = sem("decay_scanned")
        split_step = sem("split_step")
        lhs_ready = sem("lhs_ready")
        chunk_end_ready = sem("chunk_end_ready")
        rhs_placed = sem("rhs_placed")
        q_ready = sem("q_ready")
        k_ready = sem("k_ready")
        g_ready = sem("g_ready")
        v_ready = sem("v_ready")
        qsq_ready = sem("qsq_ready")
        qT_ready = sem("qT_ready")
        qsum_ready = sem("qsum_ready")
        qeps_hi_ready = sem("qeps_hi_ready")
        qeps_lo_ready = sem("qeps_lo_ready")
        q_placed = sem("q_placed")
        kT_ready = sem("kT_ready")
        gcopy_ready = sem("gcopy_ready")
        gmin_ready = sem("gmin_ready")
        gabs_ready = sem("gabs_ready")
        gexp_ready = sem("gexp_ready")
        gln_ready = sem("gln_ready")
        gsig_ready = sem("gsig_ready")
        vsq_ready = sem("vsq_ready")
        ktok_ready = sem("ktok_ready")
        ksq_ready = sem("ksq_ready")
        kvlog_ready = sem("kvlog_ready")
        kvlog_sum = sem("kvlog_sum")
        kvrms_ready = sem("kvrms_ready")
        vpad_ready = sem("vpad_ready")
        e_ready = sem("e_ready")
        decayT_ready = sem("decayT_ready")
        tail_ready = sem("tail_ready")
        ktail_ready = sem("ktail_ready")
        kdec_ready = sem("kdec_ready")
        qdec_ready = sem("qdec_ready")
        kv_ready = sem("kv_ready")
        kvnew_ready = sem("kvnew_ready")
        cdecay_ready = sem("cdecay_ready")
        state_ready = sem("state_ready")
        sdiag_act = sem("sdiag_act")
        sdiag_pool = sem("sdiag_pool")
        arg_ready = sem("arg_ready")
        decay_ready = sem("decay_ready")
        qk_ready = sem("qk_ready")
        probs_ready = sem("probs_ready")
        pv_ready = sem("pv_ready")
        osq_ready = sem("osq_ready")
        ms_ready = sem("ms_ready")
        mslog_ready = sem("mslog_ready")
        gexpo_ready = sem("gexpo_ready")
        gfac_ready = sem("gfac_ready")
        ohalf_ready = sem("ohalf_ready")
        og_ready = sem("og_ready")
        wo_ready = sem("wo_ready")
        attn_ready = sem("attn_ready")
        x1_ready = sem("x1_ready")
        ln2_stat = sem("ln2_stat")
        ln2_log = sem("ln2_log")
        rstd2_ready = sem("rstd2_ready")
        z2_ready = sem("z2_ready")
        z2T_ready = sem("z2T_ready")
        h2T_ready = sem("h2T_ready")
        shift_ready = sem("shift_ready")
        shift1_ready = sem("shift1_ready")
        xk0_ready = sem("xk0_ready")
        xk_ready = sem("xk_ready")
        xr_ready = sem("xr_ready")
        fk_ready = sem("fk_ready")
        relu_ready = sem("relu_ready")
        act_ready = sem("act_ready")
        fr_ready = sem("fr_ready")
        rabs_ready = sem("rabs_ready")
        rmin_ready = sem("rmin_ready")
        rexp_ready = sem("rexp_ready")
        rln_ready = sem("rln_ready")
        rsig_ready = sem("rsig_ready")
        r_ready = sem("r_ready")
        wv_ready = sem("wv_ready")
        fv_ready = sem("fv_ready")
        ffn_ready = sem("ffn_ready")
        y_ready = sem("y_ready")

        block = ctx.enter_context(nc.Block())

        def need(eng, s, per, i, k=None):
            value = per * i + (per if k is None else k)
            if isinstance(value, int) and value <= 0:
                return
            eng.wait_ge(s, value)

        def schedule(eng, body):
            body(0, True, False)
            body(1, True, True)
            with eng.Fori(2, B - 1) as i:
                body(i, True, True)
            body(B - 1, True, True, following=False)
            body(B, False, True)


        def first(i):
            return isinstance(i, int) and i == 0

        def rhs_constants(engine, heads):
            shape = [P, HPH, CHUNKS, CHUNK]
            engine.tensor_tensor(arg_rhs[:, heads, :].rearrange("p h (n c) -> p h n c", c=CHUNK),
                                 mask_rhs1[:].unsqueeze(1).unsqueeze(1).to_broadcast(shape),
                                 head_sel[:, ::DH][:, heads].unsqueeze(2).unsqueeze(3).to_broadcast(shape),
                                 ALU.add).then_inc(s_rhs0, 1)

        def element(dram, i):
            return dram[i:i + 1] if isinstance(i, int) else dram[bass.ds(i, 1)]

        def tokens(dram, i):
            return element(dram, i).rearrange("b p t d -> (b p) t d")

        def columns(dram, i, a, b):
            return element(dram, i)[:, :, a:b].rearrange("b p k -> (b p) k")

        def gate_row(i, a, b):
            return element(gate_dram, i)[:, a:b].rearrange("b d -> (b d)").partition_broadcast(P)

        @block.sync
        def _(sp):
            sp.dma_start(cT_sb[:], cT.rearrange("(k p) n -> p k n", p=P)).then_inc(s_wmod, 16)
            sp.dma_start(wmod_sb, wmod.rearrange("(k p) n -> p k n", p=P)).then_inc(s_wmod, 16)
            sp.dma_start(x_in[:], tokens(x_tiles, 0)).then_inc(x_loaded, 16)
            for dst, src in ((w_gt16[:], Wgt), (w_staged[:, 0], Wq), (w_staged[:, 1], Wk), (w_staged[:, 2], Wg),
                             (w_staged[:, 3], Wv), (w_o[:], Wo), (w_r[:], WrT), (w_fk[:], WkT), (w_fv[:], WvT)):
                sp.dma_start(dst, src.rearrange("(k p) n -> p k n", p=P)).then_inc(s_w, 16)
            for n, src in enumerate((mu_r, mu_k)):
                sp.dma_start(mu[:, n, :], src.rearrange("(k p) -> p k", p=P), allow_slow_non_contiguous=True).then_inc(s_w, 16)
            sp.wait_ge(s_modt, 4)
            sp.dma_start(mod_dram.rearrange("b p k -> p b k"), mod_all).then_inc(s_modw, 16)
            sp.wait_ge(s_mods, 6)
            sp.dma_start(gate_dram, gate_rows).then_inc(s_modw, 16)
            sp.wait_ge(s_modw, 32)
            sp.dma_start(gate_a[:], gate_row(0, 0, D)).then_inc(gatea_loaded, 16)
            sp.wait_ge(s_zero, 3)

            def body(i, attn, later, following=True):
                j = i - 1
                if attn:
                    if following:
                        need(sp, z_ready, 4, i)
                        sp.dma_start(x_in[:], tokens(x_tiles, i + 1)).then_inc(x_loaded, 16)
                        need(sp, hT_ready, 2, i)
                        sp.dma_start(mod_a[:], columns(mod_dram, i + 1, 0, 4)).then_inc(moda_loaded, 16)
                    need(sp, qk_ready, 4, i - 1)
                    need(sp, qT_ready, 1, i)
                    for h in range(HPH):
                        rows = slice(DH * h, DH * (h + 1))
                        sp.dma_start(q_diag[rows, :, h, :], qT[rows, :, :]).then_inc(q_placed, 16)
                    need(sp, arg_ready, 4, i - 1)
                    need(sp, split_step, 5, i)
                    if first(i):
                        sp.wait_ge(s_rhs0, 2)
                    for r in PART_ROWS:
                        sp.dma_start(arg_rhs[r + HEADS:r + HEADS + 1, :, :],
                                     split[r:r + HEADS, :]).then_inc(rhs_placed, 16)
                    if following:
                        need(sp, wo_ready, 1, i)
                        sp.dma_start(gate_a[:], gate_row(i + 1, 0, D)).then_inc(gatea_loaded, 16)
                    need(sp, h2T_ready, 2, j)
                    sp.dma_start(mod_f[:], columns(mod_dram, i, 4, 8)).then_inc(modf_loaded, 16)
                    need(sp, wv_ready, 1, j)
                    sp.dma_start(gate_f[:], gate_row(i, D, 2 * D)).then_inc(gatef_loaded, 16)
                if later:
                    need(sp, y_ready, 1, j)
                    sp.dma_start(tokens(out_tiles, j), ffn[:]).then_inc(stored, 16)
                if attn:
                    sp.dma_start(x1[:], tokens(x_tiles, i)).then_inc(xres_loaded, 16)

            schedule(sp, body)
            sp.wait_ge(stored, 16 * B)

        @block.gpsimd
        def _(pool):
            g = nc.gpsimd
            g.memset(ident[:], 0.0).then_inc(s_pc, 1)
            g.memset(mask_lhs1[:], 0.0).then_inc(s_pc, 1)
            g.memset(mask_rhs1[:], 0.0).then_inc(s_pc, 1)
            g.memset(head_sel[:], 0.0).then_inc(s_pc, 1)
            g.memset(head_mean[:], 1.0 / DH).then_inc(s_pc, 1)
            g.memset(lhs_scale[:], 0.0).then_inc(s_pc, 1)
            made = [6]

            def select(part, op, fill, base, pattern, row_step):
                pool.wait_ge(s_pc, made[0])
                g.affine_select(out=part, in_=part, compare_op=op, fill=fill, base=base, pattern=pattern,
                                channel_multiplier=row_step).then_inc(s_pc, 1)
                made[0] += 1

            select(ident[:], ALU.not_equal, 1.0, 0, [[-1, P]], 1)
            for r, first in MASK_ROWS:
                select(mask_lhs1[r:r + 32, :], ALU.is_ge, MASKED, first, [[-1, CHUNK]], 1)
                select(mask_rhs1[r:r + 32, :], ALU.not_equal, 1.0, first, [[-1, CHUNK]], 1)
                if r in PART_ROWS:
                    for m in (mask_lhs1, mask_rhs1):
                        select(m[r:r + 32, :], ALU.is_ge, 0.0, -(HEADS + 1), [[0, CHUNK]], 1)
                    select(mask_lhs1[r:r + 32, :], ALU.not_equal, 1.0, -HEADS, [[0, CHUNK]], 1)
            for r in PART_ROWS:
                part = head_sel[r:r + 32, :].rearrange("p (h d) -> p h d", h=HEADS)
                select(part, ALU.not_equal, 1.0, 0, [[-1, HEADS], [0, DH]], 1)
                select(lhs_scale[r:r + 32, :], ALU.is_ge, -1.0, -HEADS, [[0, 1]], 1)
            blocks = head_mean[:].rearrange("p (h d) -> p h d", h=HPH)
            select(blocks, ALU.is_ge, 0.0, 0, [[-DH, HPH], [0, DH]], 1)
            select(blocks, ALU.is_ge, 0.0, DH - 1, [[DH, HPH], [0, DH]], -1)
            pool.wait_ge(s_pc, POOL_CONSTANTS)
            g.memset(v_pad[:], 0.0).then_inc(s_zero, 1)
            g.memset(state_diag[:], 0.0).then_inc(s_zero, 1)
            pool.wait_ge(s_modp, 1)
            g.memset(q_diag[:], 0.0).then_inc(s_zero, 1)
            rhs_constants(g, slice(HPH, HEADS))
            pool.wait_ge(s_zero, 3)
            pool.wait_ge(s_w, 16 * WEIGHT_LOADS)
            pool.wait_ge(s_vc, VECTOR_CONSTANTS)
            pool.wait_ge(s_modw, 32)

            def body(i, attn, later, following=True):
                j = i - 1
                if attn:
                    need(pool, qT_ready, 1, i)
                    need(pool, ms_ready, 2, j)
                    need(pool, kv_ready, 1, i - 1)
                    g.tensor_tensor(q_sq, qT[:, 0, :], qT[:, 0, :], ALU.mult).then_inc(qsq_ready, 1)
                    g.tensor_tensor(q_sq1, qT[:, 1, :], qT[:, 1, :], ALU.mult).then_inc(qsq_ready, 1)
                    need(pool, qsq_ready, 2, i)
                    g.tensor_tensor(q_sq, q_sq, q_sq1,
                                    ALU.add).then_inc(qsum_ready, 1)
                    need(pool, gatea_loaded, 16, i)
                    need(pool, attn_ready, 2, j)
                    g.tensor_tensor(w_o_gated[:], w_o[:],
                                    gate_a[:].unsqueeze(1).to_broadcast([P, HALVES, D]),
                                    ALU.mult).then_inc(wo_ready, 1)
                if later:
                    need(pool, gatef_loaded, 16, j)
                    need(pool, fv_ready, 2, j - 1)
                    g.tensor_tensor(w_fv_gated[:], w_fv[:],
                                    gate_f[:].unsqueeze(1).to_broadcast([P, HALVES, D]),
                                    ALU.mult).then_inc(wv_ready, 1)
                if later and attn:
                    need(pool, h2T_ready, 2, j, 1)
                    g.tensor_tensor(shift_d[:, 0, :], h2T[:, 0, 1:T + 1], h2T[:, 0, 0:T],
                                    ALU.subtract).then_inc(shift_ready, 1)
                    need(pool, relu_ready, 2, j)
                    g.tensor_tensor(act_T[:], act_T[:], act_T[:], ALU.mult).then_inc(act_ready, 1)
                if attn:
                    need(pool, state_ready, 1, i)
                    need(pool, pv_ready, 4, i - 1)
                    need(pool, wo_ready, 1, i)
                    if later:
                        need(pool, act_ready, 1, j)
                    for q in (2, 3):
                        if q == 3:
                            need(pool, sdiag_pool, 2, i, 1)
                        rows = slice(32 * q, 32 * q + 32)
                        g.tensor_tensor(
                            state_diag[rows, :, 1:CHUNKS, 32 * q:32 * q + 32],
                            state[rows, :, :, 0:CHUNKS - 1].rearrange("p a e n -> p a n e"),
                            one[rows, :].unsqueeze(1).unsqueeze(1).to_broadcast([32, HALVES, CHUNKS - 1, 32]),
                            ALU.mult).then_inc(sdiag_pool, 1)
                    need(pool, sdiag_pool, 2, i)
                    need(pool, gmin_ready, 1, i)
                    need(pool, gln_ready, 1, i)
                    g.tensor_tensor(g_log[:], g_log[:], g_exp[:], ALU.subtract).then_inc(gsig_ready, 1)
                if later and attn:
                    need(pool, rmin_ready, 1, j)
                    need(pool, rln_ready, 1, j)
                    g.tensor_tensor(r_min[:], r_min[:], r_exp, ALU.subtract).then_inc(rsig_ready, 1)
                    need(pool, ffn_ready, 1, j)
                    g.tensor_tensor(ffn[:], ffn[:], x1[:], ALU.add).then_inc(y_ready, 1)

            schedule(pool, body)

        @block.scalar
        def _(act):
            a = nc.scalar
            a.preload_act_table_set("natural_log_exp_and_others")
            act.wait_ge(s_wmod, 32)
            a.activation(c_tmp[:], cT_sb[:], ACT.Exp, scale=-1.0).then_inc(s_c1, 1)

            def body(i, attn, later, following=True):
                j = i - 1
                if later:
                    need(act, pv_ready, 4, j)
                    a.activation(o_sq[:], bank(4, 2), ACT.Square).then_inc(osq_ready, 1)
                if attn:
                    need(act, moda_loaded, 16, i)
                    need(act, g_ready, 2, i - 1)
                    need(act, fr_ready, 2, j - 1)
                    for half in range(HALVES):
                        need(act, zT_ready, 2, i, half + 1)
                        a.activation(hT[:, half, :], bank(half), ACT.Identity,
                                     scale=mod_a[:, half:half + 1],
                                     bias=mod_a[:, 2 + half:3 + half]).then_inc(hT_ready, 1)
                        need(act, hT_ready, 2, i, half + 1)
                        a.activation(h_hi[:, half, :], hT[:, half, :], ACT.Copy).then_inc(hhi_ready, 1)
                if later:
                    need(act, gsig_ready, 1, j)
                    need(act, rsig_ready, 1, j - 1)
                    for half in range(HALVES):
                        need(act, ms_ready, 2, j, half + 1)
                        a.activation(g_exp[:, half, :], bank(2 + half)[:, 0, :], ACT.Ln,
                                     bias=eps_out[:]).then_inc(mslog_ready, 1)
                    for half in range(HALVES):
                        need(act, gexpo_ready, 2, j, half + 1)
                        a.activation(g_log[:, half, :], g_log[:, half, :], ACT.Exp).then_inc(gfac_ready, 1)
                if attn:
                    need(act, gt_ready, 1, i)
                    need(act, state_ready, 1, j)
                    a.activation(gt_b[:], bank(6)[:, 0, :], ACT.Abs).then_inc(gt_abs, 1)
                    need(act, gt_abs, 1, i)
                    a.activation(gt_b[:], gt_b[:], ACT.Exp, scale=-1.0).then_inc(gt_exp, 1)
                    need(act, gt_exp, 1, i)
                    a.activation(gt_b[:], gt_b[:], ACT.Ln, bias=one[:]).then_inc(gt_log, 1)
                    need(act, q_ready, 2, i)
                    a.activation(qT[:], bank(0, 2), ACT.Copy).then_inc(qT_ready, 1)
                    if first(i):
                        act.wait_ge(s_wlo, 4)
                        act.wait_ge(s_modw, 32)
                    need(act, qk_ready, 4, i - 1)
                    copy_k(i, 0)
                    copy_k(i, 1)
                if later:
                    need(act, ln2_stat, 8, j)
                    a.activation(rstd2[:], ln2_mv[:, :, 1], ACT.Ln, bias=eps_ln[:]).then_inc(ln2_log, 1)
                    need(act, ln2_log, 1, j)
                    a.activation(rstd2[:], rstd2[:], ACT.Exp, scale=-0.5).then_inc(rstd2_ready, 1)
                if attn:
                    need(act, split_step, 5, i)
                    need(act, tail_ready, 1, i - 1)
                    a.activation(chunk_end[:].rearrange("p (n c) -> p n c", c=CHUNK),
                                 split[:, CHUNK - 1::CHUNK].unsqueeze(2).to_broadcast([P, CHUNKS, CHUNK]),
                                 ACT.Copy).then_inc(chunk_end_ready, 1)
                    need(act, qsum_ready, 1, i)
                    a.activation(q_eps[:, 0, :], q_sq, ACT.Copy, scale=EPS_MEAN).then_inc(qeps_hi_ready, 1)
                    need(act, tail_ready, 1, i)
                    a.activation(k_tail[:], bank(7)[:, 0, 0:TILES * HEADS], ACT.Exp,
                                 scale=1.0 / GATE_NORM).then_inc(ktail_ready, 1)
                    need(act, kvlog_sum, 1, i - 1)
                    for t in (0, 1):
                        need(act, v_ready, 2, i, t // 2 + 1)
                        a.activation(sq_junk[:, t, :], bank(4 + t // 2)[:, 0, (t % 2) * D:(t % 2 + 1) * D],
                                     ACT.Square, accum_out=kv_sumsq[:, 0, t:t + 1]).then_inc(vsq_ready, 1)
                    need(act, e_ready, 2, i)
                    need(act, attn_ready, 2, j)
                    a.activation(decay_T, bank(0, 2), ACT.Exp, scale=1.0 / GATE_NORM).then_inc(decayT_ready, 1)
                if later:
                    second_modulated(j, 0)
                    second_modulated(j, 1)
                if attn:
                    for t in (2, 3):
                        need(act, v_ready, 2, i, t // 2 + 1)
                        a.activation(sq_junk[:, t, :], bank(4 + t // 2)[:, 0, (t % 2) * D:(t % 2 + 1) * D],
                                     ACT.Square, accum_out=kv_sumsq[:, 0, t:t + 1]).then_inc(vsq_ready, 1)
                    for t in range(TILES):
                        need(act, ktok_ready, 2, i, t // 2 + 1)
                        a.activation(sq_junk[:, TILES + t, :], bank(2 + t // 2)[:, 0, (t % 2) * D:(t % 2 + 1) * D],
                                     ACT.Square, accum_out=kv_sumsq[:, 1, t:t + 1]).then_inc(ksq_ready, 1)
                if attn:
                    need(act, vsq_ready, 4, i)
                    need(act, ksq_ready, 4, i)
                    a.activation(kv_sumsq[:], kv_sumsq[:], ACT.Ln, scale=1.0 / D,
                                 bias=eps_rms[:]).then_inc(kvlog_ready, 1)
                    need(act, kvlog_sum, 1, i)
                    need(act, vpad_ready, 4, i - 1)
                    a.activation(kv_rms8[:], kv_rms[:].unsqueeze(2).to_broadcast([P, TILES, 8]),
                                 ACT.Exp, scale=-0.5).then_inc(kvrms_ready, 1)
                    need(act, decayT_ready, 1, i)
                    need(act, state_ready, 1, i - 1)
                    for half in range(HALVES):
                        a.activation(chunk_decay[:, half, :, 1:CHUNKS],
                                     decay_T[:, half, 2 * CHUNK - 1::CHUNK].unsqueeze(1).to_broadcast(
                                         [P, 32, CHUNKS - 1]), ACT.Copy).then_inc(cdecay_ready, 1)
                if later:
                    need(act, xk_ready, 2, j)
                    need(act, xr_ready, 2, j)
                    for half in range(HALVES):
                        need(act, fk_ready, 2, j, half + 1)
                        a.activation(act_T[:, half, :], bank(6 + half)[:, 0, :],
                                     ACT.Relu).then_inc(relu_ready, 1)
                if attn:
                    need(act, gcopy_ready, 1, i)
                    need(act, gexpo_ready, 2, j)
                    a.activation(g_exp[:], g_copy[:], ACT.Abs).then_inc(gabs_ready, 1)
                    for t in range(TILES):
                        need(act, arg_ready, 4, i, t + 1)
                        if t == 0:
                            need(act, qdec_ready, 1, i)
                            need(act, cdecay_ready, 2, i)
                        need(act, probs_ready, 4, i, t - 1)
                        a.activation(decay[:, t % 2, :].rearrange("p (b n) -> p b n", b=2), bank(0, 2),
                                     ACT.Exp, scale=1.0 / GATE_NORM).then_inc(decay_ready, 1)
                        if t == 0:
                            need(act, gabs_ready, 1, i)
                            a.activation(g_exp[:], g_exp[:], ACT.Exp, scale=-1.0).then_inc(gexp_ready, 1)
                            need(act, gexp_ready, 1, i)
                            a.activation(g_exp[:], g_exp[:], ACT.Ln, bias=one[:]).then_inc(gln_ready, 1)
                            need(act, state_ready, 1, i)
                            need(act, pv_ready, 4, i - 1)
                            for q in (0, 1):
                                rows = slice(32 * q, 32 * q + 32)
                                for half in range(HALVES):
                                    a.activation(
                                        state_diag[rows, half, 1:CHUNKS, 32 * q:32 * q + 32],
                                        state[rows, half, :, 0:CHUNKS - 1].rearrange("p e n -> p n e"),
                                        ACT.Copy).then_inc(sdiag_act, 1)
                        if t == 1 and later:
                            need(act, gsig_ready, 1, i)
                            receptance_log(j)
                        if t == 2 and following:
                            first_rstd(i + 1)
                        if t == 2 and later:
                            receptance(j)
                elif later:
                    receptance_log(j)
                    receptance(j)

            def copy_k(i, half):
                need(act, k_ready, 2, i, half + 1)
                a.activation(kT[:, half, :], bank(half)[:, 0, :], ACT.Copy).then_inc(kT_ready, 1)

            def second_modulated(j, half):
                need(act, modf_loaded, 16, j)
                need(act, xr_ready, 2, j - 1)
                need(act, xk_ready, 2, j - 1)
                need(act, z2T_ready, 2, j, half + 1)
                a.activation(h2T[:, half, 1:T + 1], bank(6 + half), ACT.Identity,
                             scale=mod_f[:, half:half + 1],
                             bias=mod_f[:, 2 + half:3 + half]).then_inc(h2T_ready, 1)

            def first_rstd(i):
                need(act, ln_stat, 8, i)
                a.activation(rstd[:], ln_mv[:, :, 1], ACT.Ln, bias=eps_ln[:]).then_inc(ln_log, 1)
                need(act, ln_log, 1, i)
                a.activation(rstd[:], rstd[:], ACT.Exp, scale=-0.5).then_inc(rstd_ready, 1)

            def receptance_log(j):
                need(act, fr_ready, 2, j)
                a.activation(g_exp[:], bank(6, 2), ACT.Abs).then_inc(rabs_ready, 1)
                need(act, rabs_ready, 1, j)
                a.activation(r_exp, r_exp, ACT.Exp, scale=-1.0).then_inc(rexp_ready, 1)
                need(act, rexp_ready, 1, j)
                a.activation(r_exp, r_exp, ACT.Ln, bias=one[:]).then_inc(rln_ready, 1)

            def receptance(j):
                need(act, rsig_ready, 1, j)
                a.activation(r_min[:], r_min[:], ACT.Exp).then_inc(r_ready, 1)

            first_rstd(0)
            act.wait_ge(s_modp, 1)
            for n in range(2):
                a.activation(mod_rows[:, n * 2 * D:(n + 1) * 2 * D], bank(6 + n)[0:B, 0, :],
                             ACT.Copy).then_inc(s_modr, 1)
            act.wait_ge(s_w, 16 * WEIGHT_LOADS)
            for n, w in enumerate((w_q, w_k, w_g, w_v)):
                a.activation(w[:, 0], w_staged[:, n], ACT.Copy).then_inc(s_whi, 1)
            act.wait_ge(s_pc, POOL_CONSTANTS)
            act.wait_ge(s_vc, VECTOR_CONSTANTS)
            schedule(act, body)

        @block.tensor
        def _(pe):
            mm = nc.tensor.matmul

            def ffn_key(j, half):
                for k in range(HALVES):
                    need(pe, xk_ready, 2, j, k + 1)
                    last = mm(bank(6 + half)[:, 0, :], w_fk[:, k, half * P:(half + 1) * P], xkT[:, k, :],
                              start=(k == 0), stop=(k == HALVES - 1))
                last.then_inc(fk_ready, 1)

            def split_passes():
                passes = [(w, h_hi, k) for k in range(HALVES) for w in range(2)]
                passes += [(0, h_lo, k) for k in range(HALVES)]
                return [(n == 0, n == len(passes) - 1) + p for n, p in enumerate(passes)]

            def project_h(dst, weight, done):
                for begin, end, w, x, k in split_passes():
                    last = mm(dst, weight(w, k), x[:, k, :], start=begin, stop=end)
                last.then_inc(done, 1)

            def transposes(src, first_bank, done):
                for half in range(HALVES):
                    for t in range(TILES):
                        last = nc.tensor.transpose(bank(first_bank + half)[:, 0, t * P:(t + 1) * P],
                                                   src[:, t, half * P:(half + 1) * P], ident[:])
                    last.then_inc(done, 1)

            pe.wait_ge(s_wmod, 32)
            pe.wait_ge(s_c2, 3)
            for dst, cols in ((bank(6)[0:B, 0, :], 0), (bank(7)[0:B, 0, :], 3 * D),
                              (bank(2)[0:B, 0, 0:D], 2 * D), (bank(2)[0:B, 0, D:2 * D], 5 * D)):
                width = dst.shape[-1]
                for k in range(HALVES):
                    last = mm(dst, c_silu[:, k, :], wmod_sb[:, k, cols:cols + width],
                              start=(k == 0), stop=(k == HALVES - 1))
            last.then_inc(s_modp, 1)
            pe.wait_ge(s_pc, POOL_CONSTANTS)
            pe.wait_ge(s_modr, 2)
            for m in range(8):
                last = nc.tensor.transpose(bank(3)[:, 0, m * B:(m + 1) * B], mod_rows[:, m * P:(m + 1) * P],
                                           ident[0:B, 0:B])
            last.then_inc(s_modf, 1)
            pe.wait_ge(s_w, 16 * WEIGHT_LOADS)
            pe.wait_ge(s_vc, VECTOR_CONSTANTS)

            def attend(i, t):
                need(pe, probs_ready, 4, i, t + 1)
                if t == 0:
                    need(pe, kvnew_ready, 1, i)
                    need(pe, kdec_ready, 2, i)
                    need(pe, qdec_ready, 1, i)
                    need(pe, sdiag_act, 4, i)
                    need(pe, sdiag_pool, 2, i)
                for half in range(HALVES):
                    for c in range(2):
                        n = 2 * t + c
                        cols = slice(n * CHUNK, (n + 1) * CHUNK)
                        for step in range(3 if n else 2):
                            for q in range(PAIRS):
                                dst = bank(4 + half)[32 * q:32 * q + 32, 0, cols]
                                if step < 2:
                                    h = half * HPH + 2 * q + step
                                    last = mm(dst, v_pad[:, c, t, h, :],
                                              probs[:, t % 2, h * CHUNK:(h + 1) * CHUNK],
                                              start=(step == 0), stop=(step == 1 and n == 0))
                                else:
                                    last = mm(dst, state_diag[:, half, n, 32 * q:32 * q + 32],
                                              q_dec[:, half, cols], start=False, stop=True)
                last.then_inc(pv_ready, 1)

            def body(i, attn, later, following=True):
                j = i - 1
                if attn:
                    need(pe, z_ready, 4, i)
                    need(pe, decay_ready, 4, i - 1)
                    transposes(z, 0, zT_ready)
                if later:
                    need(pe, qeps_hi_ready, 1, j)
                    need(pe, qeps_lo_ready, 1, j)
                    need(pe, probs_ready, 4, j)
                    for half in range(HALVES):
                        for part in range(2):
                            mm(bank(2 + half)[:, 0, :], ones[:], q_eps[:, part, :], start=(part == 0),
                               stop=False, skip_group_check=True)
                    need(pe, osq_ready, 1, j)
                    for half in range(HALVES):
                        mm(bank(2 + half)[:, 0, :], head_mean[:], o_sq[:, half, :], start=False,
                           stop=True, skip_group_check=True).then_inc(ms_ready, 1)
                if attn:
                    need(pe, ffn_ready, 1, j - 1)
                    if first(i):
                        pe.wait_ge(s_wlo, 4)
                    for begin, end, w, h, k in split_passes():
                        need(pe, hhi_ready, 2, i, k + 1)
                        if h is h_lo:
                            need(pe, hlo_ready, 2, i, k + 1)
                        last = mm(bank(6)[:, 0, :], w_gt[:, w, k].rearrange("p r h -> p (r h)"), h[:, k, :],
                                  start=begin, stop=end)
                    last.then_inc(gt_ready, 1)
                    for half in range(HALVES):
                        project_h(bank(half)[:, 0, :],
                                  lambda w, k: w_q[:, w, k, half * P:half * P + P], q_ready)
                if later:
                    need(pe, og_ready, 2, j)
                    need(pe, wo_ready, 1, j)
                    need(pe, mslog_ready, 2, j)
                    for t in range(TILES):
                        for k in range(HALVES):
                            last = mm(bank(2 + t // 2)[:, 0, (t % 2) * D:(t % 2 + 1) * D],
                                      o_gated[:, k, t * P:(t + 1) * P], w_o_gated[:, k, :],
                                      start=(k == 0), stop=(k == HALVES - 1))
                        if t % 2:
                            last.then_inc(attn_ready, 1)
                if attn:
                    need(pe, qT_ready, 1, i)
                    for half in range(HALVES):
                        project_h(bank(half)[:, 0, :],
                                  lambda w, k: w_k[:, w, k, half * P:half * P + P], k_ready)
                    need(pe, ohalf_ready, 1, j)
                    for t in range(TILES):
                        for begin, end, w, h, k in split_passes():
                            last = mm(bank(4 + t // 2)[:, 0, (t % 2) * D:(t % 2 + 1) * D],
                                      h[:, k, t * P:(t + 1) * P], w_v[:, w, k, :], start=begin, stop=end)
                        if t % 2:
                            last.then_inc(v_ready, 1)
                    tails(i)
                    need(pe, kT_ready, 2, i)
                    for half in range(HALVES):
                        mm(bank(half)[:, 0, :], head_sel[:, half * P:(half + 1) * P], split[:],
                           start=True, stop=True).then_inc(e_ready, 1)
                if later:
                    need(pe, z2_ready, 4, j)
                    if attn:
                        need(pe, ktail_ready, 1, i)
                        need(pe, gt_min, 1, i)
                    else:
                        need(pe, ffn_ready, 1, j - 1)
                    transposes(z2, 6, z2T_ready)
                if attn:
                    need(pe, x1_ready, 2, j)
                    if first(i):
                        pe.wait_ge(s_mods, 6)
                    for t in range(TILES):
                        for half in range(HALVES):
                            last = nc.tensor.transpose(
                                bank(2 + t // 2)[:, 0, (t % 2) * D + half * P:(t % 2) * D + half * P + P],
                                kT[:, half, t * P:(t + 1) * P], ident[:])
                        if t % 2:
                            last.then_inc(ktok_ready, 1)
                if attn:
                    need(pe, decayT_ready, 1, i)
                    for half in range(HALVES):
                        project_h(bank(half)[:, 0, :],
                                  lambda w, k: w_g[:, w, k, half * P:half * P + P], g_ready)
                if later:
                    for half in range(HALVES):
                        ffn_key(j, half)
                    if not attn:
                        receptance_logits(j, 0)
                        receptance_logits(j, 1)
                if attn:
                    need(pe, vpad_ready, 4, i)
                    need(pe, kdec_ready, 2, i)
                    for half in range(HALVES):
                        for t in range(TILES):
                            for c in range(2):
                                for q in range(PAIRS):
                                    rows = slice(32 * q, 32 * q + 32)
                                    n = half * CHUNKS + 2 * t + c
                                    h = half * HPH + 2 * q
                                    v = v_pad[:, c, t, h:h + 2, :].rearrange("p h e -> p (h e)")
                                    rhs = pair_values(v)
                                    last = mm(bank(4)[rows, 0, n * 32:n * 32 + 32],
                                              k_dec[:, t, half * P + 32 * q:half * P + 32 * q + 32], rhs,
                                              start=True, stop=True)
                    last.then_inc(kv_ready, 1)
                    for t in range(TILES):
                        need(pe, lhs_ready, 1, i)
                        need(pe, rhs_placed, 16 * len(PART_ROWS), i)
                        if t == 0:
                            need(pe, gcopy_ready, 1, i)
                        else:
                            need(pe, decay_ready, 4, i, t)
                        for half in range(HALVES):
                            for c in range(2):
                                cols = slice((2 * t + c) * CHUNK, (2 * t + c + 1) * CHUNK)
                                last = mm(bank(half)[CHUNK * c:CHUNK * (c + 1), 0, :].rearrange(
                                              "p (h n) -> p h n", h=HPH),
                                          arg_lhs[:, cols],
                                          arg_rhs[:, half * HPH:(half + 1) * HPH, cols],
                                          start=True, stop=True)
                        last.then_inc(arg_ready, 1)
                        if t == 1 and later:
                            receptance_logits(j, 1)
                        if t == 0:
                            need(pe, q_placed, 16 * HPH, i)
                            need(pe, kdec_ready, 2, i)
                        else:
                            need(pe, probs_ready, 4, i, t)
                        for half in range(HALVES):
                            for c in range(2):
                                cols = slice((2 * t + c) * CHUNK, (2 * t + c + 1) * CHUNK)
                                last = mm(bank(2 + half)[CHUNK * c:CHUNK * (c + 1), 0, :].rearrange(
                                              "p (h n) -> p h n", h=HPH),
                                          kT[:, half, cols], q_diag[:, half, :, cols],
                                          start=True, stop=True)
                        last.then_inc(qk_ready, 1)
                        if t == 0 and later:
                            receptance_logits(j, 0)
                        if t >= 1:
                            attend(i, t - 1)
                        if t == 2 and later:
                            ffn_value(j)
                    attend(i, TILES - 1)
                elif later:
                    ffn_value(j)

            def tails(i):
                need(pe, chunk_end_ready, 1, i)
                need(pe, split_step, 5, i)
                for t in range(TILES):
                    cols = slice(t * P, (t + 1) * P)
                    dst = bank(7)[:, 0, t * HEADS:(t + 1) * HEADS]
                    mm(dst, split[:, cols], head_sel_neg[:], start=True, stop=False)
                    last = mm(dst, chunk_end[:, cols], head_sel[:, ::DH], start=False, stop=True)
                last.then_inc(tail_ready, 1)

            def receptance_logits(j, pair):
                need(pe, xr_ready, 2, j)
                need(pe, relu_ready, 2, j, pair + 1)
                for t in (2 * pair, 2 * pair + 1):
                    for k in range(HALVES):
                        last = mm(bank(6 + pair)[:, 0, (t % 2) * D:(t % 2 + 1) * D],
                                  xrT[:, k, t * P:(t + 1) * P], w_r[:, k, :],
                                  start=(k == 0), stop=(k == HALVES - 1))
                last.then_inc(fr_ready, 1)

            def ffn_value(j):
                need(pe, act_ready, 1, j)
                need(pe, wv_ready, 1, j)
                need(pe, rmin_ready, 1, j)
                for t in range(TILES):
                    for k in range(HALVES):
                        last = mm(bank(6 + t // 2)[:, 0, (t % 2) * D:(t % 2 + 1) * D],
                                  act_T[:, k, t * P:(t + 1) * P], w_fv_gated[:, k, :],
                                  start=(k == 0), stop=(k == HALVES - 1))
                    if t % 2:
                        last.then_inc(fv_ready, 1)

            schedule(pe, body)

        @block.vector
        def _(dve):
            v = nc.vector
            v.memset(eps_ln[:], LN_EPS).then_inc(s_vc, 1)
            v.memset(eps_rms[:], RMS_EPS).then_inc(s_vc, 1)
            v.memset(eps_out[:], RMS_EPS * RMS_EPS * DH).then_inc(s_vc, 1)
            v.memset(ones[:].bitcast(F32), 1.0).then_inc(s_vc, 1)
            v.memset(one[:], 1.0).then_inc(s_vc, 1)
            v.memset(chunk_keep[:], 1.0).then_inc(s_vc, 1)
            v.memset(h2T[:, :, 0:1], 0.0).then_inc(s_vc, 1)
            v.memset(chunk_decay[:], 0.0).then_inc(s_vc, 1)
            dve.wait_ge(s_vc, 8)
            v.memset(chunk_keep[:, ::CHUNK], 0.0).then_inc(s_vc, 1)
            dve.wait_ge(s_c1, 1)
            v.tensor_scalar(c_tmp[:], c_tmp[:], 1.0, None, ALU.add).then_inc(s_c2, 1)
            dve.wait_ge(s_c2, 1)
            v.reciprocal(c_tmp[:], c_tmp[:]).then_inc(s_c2, 1)
            dve.wait_ge(s_c2, 2)
            dve.wait_ge(s_wmod, 32)
            v.tensor_tensor(c_silu[:], c_tmp[:], cT_sb[:], ALU.mult).then_inc(s_c2, 1)
            dve.wait_ge(s_pc, POOL_CONSTANTS)
            v.tensor_copy(lhs_const[:].rearrange("p (n c) -> p n c", c=CHUNK),
                          mask_lhs1[:].unsqueeze(1).to_broadcast([P, CHUNKS, CHUNK])).then_inc(s_vc, 1)
            v.tensor_scalar(head_sel_neg[:], head_sel[:, ::DH], -1.0, None, ALU.mult).then_inc(s_vc, 1)
            for q in range(PAIRS):
                r = slice(32 * q, 32 * q + 32)
                v.tensor_scalar(head_block[r, :], head_mean[r, r], float(DH), None, ALU.mult).then_inc(s_vc, 1)

            def modulation():
                dve.wait_ge(s_modf, 1)
                for n, (part, plus) in enumerate(((1, 1.0), (0, 0.0), (3, 1.0), (2, 0.0))):
                    v.tensor_scalar(mod_all[:, :, 2 * n:2 * n + 2],
                                    bank(3)[:, 0, part * 2 * B:(part + 1) * 2 * B].rearrange("p (m b) -> p b m", m=2),
                                    plus, None, ALU.add).then_inc(s_modt, 1)
                dve.wait_ge(s_modt, 4)
                v.tensor_copy(mod_a[:], mod_all[:, 0, 0:4]).then_inc(moda_loaded, 16)

            def gates():
                rows = bank(2)[0:B, 0, :]
                v.tensor_scalar(gate_tmp, rows, -1.0, None, ALU.mult).then_inc(s_mods, 1)
                dve.wait_ge(s_mods, 1)
                v.tensor_tensor(gate_tmp, gate_tmp, rows, ALU.max).then_inc(s_mods, 1)
                v.tensor_scalar(gate_rows, rows, 0.0, 2.0, ALU.is_ge, ALU.mult).then_inc(s_mods, 1)
                dve.wait_ge(s_mods, 3)
                v.tensor_scalar(gate_rows, gate_rows, -1.0, None, ALU.add).then_inc(s_mods, 1)
                v.tensor_scalar(gate_tmp, gate_tmp, MIN_GATE, None, ALU.max).then_inc(s_mods, 1)
                dve.wait_ge(s_mods, 5)
                v.tensor_tensor(gate_rows, gate_rows, gate_tmp, ALU.mult).then_inc(s_mods, 1)

            def norm_stats(i, src, stats, mv, stat_sem):
                for t in range(TILES):
                    v.bn_stats(stats[:, t, :], src[:, t, :]).then_inc(stat_sem, 1)
                norm_aggregate(i, stats, mv, stat_sem)

            def norm_aggregate(i, stats, mv, stat_sem):
                need(dve, stat_sem, 8, i, TILES)
                v.memset(carrier[:], 0.0)
                for t in range(TILES):
                    v.bn_aggr(mv[:, t, :], stats[:, t, :]).then_inc(stat_sem, 1)

            def norm_apply(i, src, mv, rstd_sem, rstd_t, dst, dst_sem):
                need(dve, rstd_sem, 1, i)
                for t in range(TILES):
                    v.tensor_scalar(dst[:, t, :], src[:, t, :], mv[:, t, 0:1], rstd_t[:, t:t + 1],
                                    ALU.subtract, ALU.mult).then_inc(dst_sem, 1)

            def body(i, attn, later, following=True):
                j = i - 1
                if later:
                    need(dve, osq_ready, 1, j)
                    need(dve, gcopy_ready, 1, j)
                    need(dve, probs_ready, 4, j)
                    v.tensor_tensor(o_gated, bank(4, 2), g_copy[:], ALU.mult).then_inc(ohalf_ready, 1)
                if attn:
                    need(dve, g_ready, 2, i - 1)
                    for half in range(HALVES):
                        need(dve, hhi_ready, 2, i, half + 1)
                        v.tensor_tensor(h_lo[:, half, :], hT[:, half, :], h_hi[:, half, :],
                                        ALU.subtract).then_inc(hlo_ready, 1)
                if first(i):
                    gates()
                if later:
                    need(dve, gsig_ready, 1, j)
                    for half in range(HALVES):
                        need(dve, mslog_ready, 2, j, half + 1)
                        v.scalar_tensor_tensor(out=g_log[:, half, :], in0=g_exp[:, half, :], scalar=-0.5,
                                               in1=g_log[:, half, :], op0=ALU.mult,
                                               op1=ALU.add).then_inc(gexpo_ready, 1)
                    need(dve, ohalf_ready, 1, j)
                    for half in range(HALVES):
                        need(dve, gfac_ready, 2, j, half + 1)
                        v.tensor_tensor(o_gated[:, half, :], o_gated[:, half, :], g_log[:, half, :],
                                        ALU.mult).then_inc(og_ready, 1)
                if attn:
                    need(dve, gt_abs, 1, i)
                    v.tensor_scalar(gt_a[:], bank(6)[:, 0, :], 0.0, None, ALU.min).then_inc(gt_min, 1)
                    need(dve, gt_min, 1, i)
                    need(dve, gt_log, 1, i)
                    v.tensor_tensor(gt_a[:], gt_a[:], gt_b[:], ALU.subtract).then_inc(gt_diff, 1)
                    need(dve, gt_diff, 1, i)
                    v.tensor_tensor_scan(decay_sum[:], chunk_keep[:], gt_a[:], 0.0, ALU.mult,
                                         ALU.add).then_inc(decay_scanned, 1)
                    need(dve, decay_scanned, 1, i)
                    need(dve, tail_ready, 1, i - 1)
                    need(dve, rhs_placed, 16 * len(PART_ROWS), i - 1)
                    v.tensor_copy(split[:], decay_sum[:]).then_inc(split_step, 1)
                if later:
                    residual(j, 0)
                if attn:
                    split_rest(i, 1, 64)
                if later:
                    second_stats(j, 0)
                if attn:
                    split_part(i, 2, 64)
                if later:
                    second_stats(j, 1)
                if later:
                    residual(j, 1)
                    second_stats(j, 2)
                    second_stats(j, 3)
                    norm_aggregate(j, ln2_stats, ln2_mv, ln2_stat)
                if attn:
                    split_rest(i, 3, 96)
                    split_part(i, 4, 96)
                if later:
                    need(dve, z2T_ready, 2, j - 1)
                    if attn:
                        need(dve, zT_ready, 2, i)
                    norm_apply(j, x1, ln2_mv, rstd2_ready, rstd2, z2, z2_ready)
                if attn:
                    need(dve, split_step, 5, i)
                    need(dve, arg_ready, 4, i - 1)
                    v.scalar_tensor_tensor(out=arg_lhs[:], in0=split[:], scalar=lhs_scale[:], in1=lhs_const[:],
                                           op0=ALU.mult, op1=ALU.add).then_inc(lhs_ready, 1)
                if first(i):
                    rhs_constants(v, slice(0, HPH))
                    dve.wait_ge(s_zero, 3)
                    dve.wait_ge(s_modw, 32)
                if attn:
                    need(dve, qeps_hi_ready, 1, i)
                    v.scalar_tensor_tensor(out=q_eps[:, 1, :], in0=q_sq, scalar=EPS_MEAN, in1=q_eps[:, 0, :],
                                           op0=ALU.mult, op1=ALU.subtract).then_inc(qeps_lo_ready, 1)
                if later:
                    need(dve, h2T_ready, 2, j)
                    need(dve, fv_ready, 2, j - 1)
                    v.tensor_tensor(shift_d[:, 1, :], h2T[:, 1, 1:T + 1], h2T[:, 1, 0:T],
                                    ALU.subtract).then_inc(shift1_ready, 1)
                    if not attn:
                        v.tensor_tensor(shift_d[:, 0, :], h2T[:, 0, 1:T + 1], h2T[:, 0, 0:T],
                                        ALU.subtract).then_inc(shift_ready, 1)
                    token_shift(j, 1, xkT, fk_ready, xk_ready)
                    if not attn:
                        token_shift(j, 0, xrT, fr_ready, xr_ready)
                        need(dve, relu_ready, 2, j)
                        v.tensor_tensor(act_T[:], act_T[:], act_T[:], ALU.mult).then_inc(act_ready, 1)
                if attn:
                    need(dve, ktail_ready, 1, i)
                    need(dve, ksq_ready, 4, i)
                    need(dve, kv_ready, 1, i - 1)
                    need(dve, qeps_lo_ready, 1, i)
                    decayed_k(i, 0)
                    need(dve, kvlog_ready, 1, i)
                    v.tensor_tensor(kv_rms[:], kv_sumsq[:, 0, :], kv_sumsq[:, 1, :],
                                    ALU.add).then_inc(kvlog_sum, 1)
                    decayed_k(i, 1)
                    need(dve, kvrms_ready, 1, i)
                    need(dve, pv_ready, 4, i - 1)
                    for b in range(2):
                        for c in range(2):
                            rows = slice(CHUNK * c, CHUNK * (c + 1))
                            v.tensor_tensor(
                                padded_heads(v_pad[rows, c, 2 * b:2 * b + 2, :, :]),
                                bank(4 + b)[rows, 0, :].rearrange("p (a s e) -> p a s e", s=2, e=DH),
                                kv_rms8[rows, 2 * b:2 * b + 2, :].rearrange("p t a -> p (t a)").unsqueeze(2)
                                .unsqueeze(3).to_broadcast([CHUNK, 16, 2, DH]),
                                ALU.mult).then_inc(vpad_ready, 1)
                    need(dve, g_ready, 2, i)
                    need(dve, ohalf_ready, 1, j)
                    v.tensor_copy(g_copy[:], bank(0, 2)).then_inc(gcopy_ready, 1)
                    if later:
                        token_shift(j, 0, xrT, fr_ready, xr_ready)
                    need(dve, gcopy_ready, 1, i)
                    need(dve, og_ready, 2, j)
                    v.tensor_scalar(g_log[:], g_copy[:], 0.0, None, ALU.min).then_inc(gmin_ready, 1)
                    need(dve, decayT_ready, 1, i)
                    need(dve, q_placed, 16 * HPH, i)
                    need(dve, qsq_ready, 2, i)
                    v.tensor_tensor(q_dec[:], qT[:], decay_T, ALU.mult).then_inc(qdec_ready, 1)
                    need(dve, kv_ready, 1, i)
                    v.tensor_tensor(
                        kv_new.rearrange("p a e n -> p a n e"),
                        bank(4)[:, 0, :].rearrange("p (a n e) -> p a n e", a=HALVES, n=CHUNKS),
                        head_block[:].unsqueeze(1).unsqueeze(1).to_broadcast([P, HALVES, CHUNKS, 32]),
                        ALU.mult).then_inc(kvnew_ready, 1)
                    need(dve, kvnew_ready, 1, i)
                    need(dve, cdecay_ready, 2, i)
                    need(dve, sdiag_act, 4, i - 1)
                    need(dve, sdiag_pool, 2, i - 1)
                    v.tensor_tensor_scan(state[:].rearrange("p a e n -> p (a e n)"),
                                         chunk_decay[:].rearrange("p a e n -> p (a e n)"),
                                         kv_new.rearrange("p a e n -> p (a e n)"),
                                         0.0, ALU.mult, ALU.add).then_inc(state_ready, 1)
                    for t in range(TILES):
                        need(dve, decay_ready, 4, i, t + 1)
                        need(dve, qk_ready, 4, i, t + 1)
                        need(dve, pv_ready, 4, i, t - 1)
                        v.tensor_tensor(probs[:, t % 2, :].rearrange("p (b n) -> p b n", b=2), bank(2, 2),
                                        decay[:, t % 2, :].rearrange("p (b n) -> p b n", b=2),
                                        ALU.mult).then_inc(probs_ready, 1)
                        if t == 1 and later:
                            receptance_min(j)
                        if t == 2 and following:
                            first_norm(i + 1, later)
                    if later:
                        ffn_product(j)
                elif later:
                    receptance_min(j)
                    need(dve, rmin_ready, 1, j)
                    need(dve, rln_ready, 1, j)
                    v.tensor_tensor(r_min[:], r_min[:], r_exp, ALU.subtract).then_inc(rsig_ready, 1)
                    ffn_product(j)
                    need(dve, ffn_ready, 1, j)
                    v.tensor_tensor(ffn[:], ffn[:], x1[:], ALU.add).then_inc(y_ready, 1)

            def decayed_k(i, b):
                v.tensor_tensor(
                    k_dec[:, 2 * b:2 * b + 2, :].rearrange("p t (h d) -> p (t h) d", h=HEADS),
                    bank(2 + b)[:, 0, :].rearrange("p (h d) -> p h d", d=DH),
                    k_tail[:, 2 * b * HEADS:(2 * b + 2) * HEADS].unsqueeze(2).to_broadcast(
                        [P, 2 * HEADS, DH]),
                    ALU.mult).then_inc(kdec_ready, 1)

            def residual(j, pair):
                need(dve, attn_ready, 2, j, pair + 1)
                need(dve, xres_loaded, 16, j)
                part = x1[:, 2 * pair:2 * pair + 2, :].rearrange("p t d -> p (t d)")
                v.tensor_tensor(part, bank(2 + pair)[:, 0, :], part, ALU.add).then_inc(x1_ready, 1)

            def second_stats(j, t):
                need(dve, x1_ready, 2, j, t // 2 + 1)
                v.bn_stats(ln2_stats[:, t, :], x1[:, t, :]).then_inc(ln2_stat, 1)

            def split_rest(i, step, row):
                need(dve, split_step, 5, i, step)
                v.tensor_tensor(decay_sum[row:P, :], decay_sum[row:P, :], split[row:P, :],
                                ALU.subtract).then_inc(split_step, 1)

            def split_part(i, step, row):
                need(dve, split_step, 5, i, step)
                v.tensor_copy(split[row:P, :], decay_sum[row:P, :]).then_inc(split_step, 1)

            def first_norm(i, later):
                need(dve, x_loaded, 16, i)
                norm_stats(i, x_in, ln_stats, ln_mv, ln_stat)
                need(dve, zT_ready, 2, i - 1)
                if later:
                    need(dve, z2T_ready, 2, i - 2)
                norm_apply(i, x_in, ln_mv, rstd_ready, rstd, z, z_ready)

            def token_shift(j, which, dst, used, done):
                need(dve, used, 2, j - 1)
                for half, shifted in ((0, shift_ready), (1, shift1_ready)):
                    need(dve, shifted, 1, j)
                    v.scalar_tensor_tensor(out=dst[:, half, :], in0=shift_d[:, half, :],
                                           scalar=mu[:, which, half:half + 1], in1=h2T[:, half, 0:T],
                                           op0=ALU.mult, op1=ALU.add).then_inc(done, 1)

            def receptance_min(j):
                need(dve, rabs_ready, 1, j)
                need(dve, stored, 16, j - 1)
                v.tensor_scalar(r_min[:].rearrange("p (b t) d -> p b (t d)", b=2), bank(6, 2), 0.0, None,
                                ALU.min).then_inc(rmin_ready, 1)

            def ffn_product(j):
                need(dve, fv_ready, 2, j)
                need(dve, r_ready, 1, j)
                v.tensor_tensor(ffn[:].rearrange("p (b t) d -> p b (t d)", b=2), bank(6, 2),
                                r_min[:].rearrange("p (b t) d -> p b (t d)", b=2),
                                ALU.mult).then_inc(ffn_ready, 1)

            first_norm(0, False)
            dve.wait_ge(s_w, 16 * WEIGHT_LOADS)
            v.tensor_copy(w_gt[:, 0], w_gt16[:].unsqueeze(2).to_broadcast([P, HALVES, 8, HEADS])).then_inc(s_vc, 1)
            dve.wait_ge(s_vc, VECTOR_CONSTANTS - 1)
            v.tensor_tensor(w_gt[:, 1], w_gt16[:].unsqueeze(2).to_broadcast([P, HALVES, 8, HEADS]), w_gt[:, 0],
                            ALU.subtract).then_inc(s_vc, 1)
            modulation()
            for n, w in enumerate((w_q, w_k, w_g, w_v)):
                dve.wait_ge(s_whi, n + 1)
                v.tensor_tensor(w[:, 1], w_staged[:, n], w[:, 0], ALU.subtract).then_inc(s_wlo, 1)
            dve.wait_ge(s_vc, VECTOR_CONSTANTS)
            schedule(dve, body)


PART_ROWS = (0, 64, 96)
MASK_ROWS = ((32, 0), (0, 32 - 17), (64, 47 - 17), (96, 62 - 17))
WEIGHT_LOADS = 11
POOL_CONSTANTS = 32
VECTOR_CONSTANTS = 17


def padded_heads(pad):
    rows = pad.shape[0]
    flat = pad.rearrange("p t (a s) e -> p (t a) (s e)", s=2)
    return bass.AP(tensor=flat.tensor, offset=flat.offset, ap=[list(flat.ap[0]), list(flat.ap[1]), [48, 2], [1, 16]])


def pair_values(pair):
    return bass.AP(tensor=pair.tensor, offset=pair.offset, ap=[list(pair.ap[0]), [48, 2], [1, 16]])


_INS = ["L0_attn_x", "L0_attn_Wq", "L0_attn_Wk", "L0_attn_Wv", "L0_attn_Wg", "L0_attn_Wgt", "L0_attn_Wo",
        "L0_ffn_W_r", "L0_ffn_W_k", "L0_ffn_W_v", "L0_ffn_mu_r", "L0_ffn_mu_k", "L0_c", "L0_wmod"]
_TRANSPOSED = {"L0_ffn_W_r", "L0_ffn_W_k", "L0_ffn_W_v", "L0_c"}


def kernel(**inputs):
    import numpy as np
    import concourse.bacc as bacc
    from concourse.bass_utils import run_bass_kernel_spmd

    nc = bacc.Bacc("TRN2", target_bir_lowering=False, num_devices=1)
    arrays, args = {}, []
    for name in _INS:
        a = np.asarray(inputs[name])
        a = np.ascontiguousarray(a.T if name in _TRANSPOSED else a)
        arrays["in_" + name] = a
        args.append(nc.dram_tensor("in_" + name, a.shape, mybir.dt.from_np(a.dtype), kind="ExternalInput").ap())
    shape = inputs["L0_attn_x"].shape
    out = nc.dram_tensor("out_0", tuple(shape), F32, kind="ExternalOutput").ap()
    adaln_block(nc, *args, out)
    r = run_bass_kernel_spmd(nc, [arrays], core_ids=[0])
    return r.results[0]["out_0"]
```
